# Optimizing a Trainium2 kernel written in Bass

```python
import numpy as np
import jax
import jax.numpy as jnp

def _softmax(x, axis=-1):
    return jax.nn.softmax(x, axis=axis)

def _gelu(x):
    return jax.nn.gelu(x, approximate=True)

def _silu(x):
    return jax.nn.silu(x)

def _sigmoid(x):
    return jax.nn.sigmoid(x)

def _layernorm(x, axis=-1, eps=1e-05):
    m = jnp.mean(x, axis=axis, keepdims=True)
    v = jnp.var(x, axis=axis, keepdims=True)
    return (x - m) / jnp.sqrt(v + eps)

def _scatter_add(tgt, idx, src, axis=0):
    return tgt.at[idx].add(src)

def _segment_sum(src, seg, n):
    return jax.ops.segment_sum(src, seg, n)
kernel_name = 'mk_flamingo_gated_d1_seqx_r8_f5e131'

def setup_inputs(seed: int=0):
    np.random.seed(seed)
    _w = jnp.asarray

    def _rec_inputs():
        import jax
        import jax.numpy as jnp
        _rk = jax.random.key(seed)
        x = -0.0003929 + 0.9999 * jax.random.normal(jax.random.fold_in(_rk, 1), (32, 100, 256), jnp.float32)
        _lenS = 100 - jax.random.randint(jax.random.fold_in(_rk, 7), (32,), 0, max(1, 100 // 4) + 1, jnp.int32)
        _lenS2 = 1444 - jax.random.randint(jax.random.fold_in(_rk, 8), (32,), 0, max(1, 1444 // 4) + 1, jnp.int32)
        _ctx_2048P = jax.random.normal(jax.random.fold_in(_rk, 11), (32, 16, 256), jnp.float32)
        _ctx_2048c = jax.random.dirichlet(jax.random.fold_in(_rk, 511), 0.3 * jnp.ones((16,), jnp.float32), (32, 1444))
        _ctx_2048t = jnp.einsum('bsk,bkd->bsd', _ctx_2048c, _ctx_2048P)
        _ctx_2048t = _ctx_2048t * jax.lax.rsqrt(jnp.mean(jnp.square(_ctx_2048t)) + 1e-12) * 0.953939
        ctx_2048 = -0.000514642 + 1.00011 * (_ctx_2048t + 0.3 * jax.random.normal(jax.random.fold_in(_rk, 611), (32, 1444, 256), jnp.float32))
        _validS = jnp.arange(100)[None, :] < _lenS[:, None]
        _validS2 = jnp.arange(1444)[None, :] < _lenS2[:, None]
        _causal = jnp.tril(jnp.ones((100, 100), dtype=bool))
        mask_BxS2_ik0 = jnp.where(jnp.broadcast_to(_validS2[:, :], (32, 1444)), 0, 1).astype(jnp.int32)
        _g = jax.random.normal(jax.random.fold_in(_rk, 9001), (2, 1), jnp.float32)
        _g = jnp.sign(_g) * jnp.maximum(jnp.abs(_g), 1.0) + (_g == 0) * 1.0
        g_xattn = _g[0]
        g_ffn = _g[1]
        return (x, ctx_2048, mask_BxS2_ik0, g_xattn, g_ffn)
    x, ctx_2048, mask_BxS2_ik0, g_xattn, g_ffn = _rec_inputs()

    def _L0_xattn_setup():
        import jax, jax.numpy as jnp
        import numpy as np
        import math
        H = 256
        NH = 16
        HD = H // NH
        EPS_LN = 1e-05
        RES_SCALE_MAX = 0.3

        def _nan_clean(x, lim=10000.0):
            return jnp.nan_to_num(x, nan=0.0, posinf=lim, neginf=-lim)
        key = jax.random.key(seed)
        ks = jax.random.split(key, 12)
        B, S, T = (4, 256, 32)
        std = 1.0 / math.sqrt(H)
        return {'hidden_states': jax.random.normal(ks[0], (B, S, H), jnp.float32), 'audio_tokens': jax.random.normal(ks[1], (B, T, H), jnp.float32), 'attention_mask': jax.random.randint(ks[2], (B, T), 0, 2, jnp.int32), 'Wq': jax.random.normal(ks[3], (H, H), jnp.float32) * std, 'bq': jnp.zeros((H,), jnp.float32), 'Wk': jax.random.normal(ks[4], (H, H), jnp.float32) * std, 'bk': jnp.zeros((H,), jnp.float32), 'Wv': jax.random.normal(ks[5], (H, H), jnp.float32) * std, 'bv': jnp.zeros((H,), jnp.float32), 'Wo': jax.random.normal(ks[6], (H, H), jnp.float32) * std, 'bo': jnp.zeros((H,), jnp.float32), 'ln_gamma': jnp.ones((H,), jnp.float32), 'ln_beta': jnp.zeros((H,), jnp.float32), 'residual_scale': jnp.float32(0.05)}
    _L0_xattn_all = _L0_xattn_setup()
    _L0_xattn_in = {k: v for k, v in _L0_xattn_all.items() if k in ('Wq', 'bq', 'Wk', 'bk', 'Wv', 'bv', 'Wo', 'bo', 'ln_gamma', 'ln_beta', 'residual_scale')}
    del _L0_xattn_all

    def _L0_ffn_setup():
        import jax, jax.numpy as jnp
        import numpy as np
        B, S, H, I, E = (2, 256, 256, 176, 8)
        TOP_K = 2
        key = jax.random.key(seed)
        k0, k1, k2, k3, k4 = jax.random.split(key, 5)
        scale = float(np.sqrt(2.0 / (H + I)))
        return {'hidden_states': jax.random.normal(k0, (B, S, H), dtype=jnp.float32), 'router_w': jax.random.normal(k1, (E, H), dtype=jnp.float32) * H ** (-0.5), 'gate_w': jax.random.normal(k2, (E, I, H), dtype=jnp.float32) * scale, 'up_w': jax.random.normal(k3, (E, I, H), dtype=jnp.float32) * scale, 'down_w': jax.random.normal(k4, (E, H, I), dtype=jnp.float32) * scale}
    _L0_ffn_all = _L0_ffn_setup()
    _L0_ffn_in = {k: v for k, v in _L0_ffn_all.items() if k in ('router_w', 'gate_w', 'up_w', 'down_w')}
    del _L0_ffn_all
    return {'x': x, 'ctx_2048': ctx_2048, 'mask_BxS2_ik0': mask_BxS2_ik0, 'g_xattn': g_xattn, 'g_ffn': g_ffn, 'L0_xattn_Wq': _L0_xattn_in['Wq'], 'L0_xattn_bq': _L0_xattn_in['bq'], 'L0_xattn_Wk': _L0_xattn_in['Wk'], 'L0_xattn_bk': _L0_xattn_in['bk'], 'L0_xattn_Wv': _L0_xattn_in['Wv'], 'L0_xattn_bv': _L0_xattn_in['bv'], 'L0_xattn_Wo': _L0_xattn_in['Wo'], 'L0_xattn_bo': _L0_xattn_in['bo'], 'L0_xattn_ln_gamma': _L0_xattn_in['ln_gamma'], 'L0_xattn_ln_beta': _L0_xattn_in['ln_beta'], 'L0_xattn_residual_scale': _L0_xattn_in['residual_scale'], 'L0_ffn_router_w': _L0_ffn_in['router_w'], 'L0_ffn_gate_w': _L0_ffn_in['gate_w'], 'L0_ffn_up_w': _L0_ffn_in['up_w'], 'L0_ffn_down_w': _L0_ffn_in['down_w']}

def reference(x, ctx_2048, mask_BxS2_ik0, g_xattn, g_ffn, L0_xattn_Wq, L0_xattn_bq, L0_xattn_Wk, L0_xattn_bk, L0_xattn_Wv, L0_xattn_bv, L0_xattn_Wo, L0_xattn_bo, L0_xattn_ln_gamma, L0_xattn_ln_beta, L0_xattn_residual_scale, L0_ffn_router_w, L0_ffn_gate_w, L0_ffn_up_w, L0_ffn_down_w):
    import jax
    import jax.numpy as jnp

    def _L0_xattn_ref(hidden_states, audio_tokens, attention_mask, Wq, bq, Wk, bk, Wv, bv, Wo, bo, ln_gamma, ln_beta, residual_scale):
        import jax, jax.numpy as jnp
        import numpy as np
        import math
        H = 256
        NH = 16
        HD = H // NH
        EPS_LN = 1e-05
        RES_SCALE_MAX = 0.3

        def _nan_clean(x, lim=10000.0):
            return jnp.nan_to_num(x, nan=0.0, posinf=lim, neginf=-lim)
        B, S, _ = hidden_states.shape
        T = audio_tokens.shape[1]
        hs = _nan_clean(hidden_states).astype(jnp.float32)
        at = _nan_clean(audio_tokens).astype(jnp.float32)

        def proj(x, W, b, L):
            y = x @ W.T + b
            return y.reshape(B, L, NH, HD).transpose(0, 2, 1, 3)
        q = _nan_clean(proj(hs, Wq, bq, S))
        k = _nan_clean(proj(at, Wk, bk, T))
        v = _nan_clean(proj(at, Wv, bv, T))
        scale = max(math.sqrt(HD), 1e-08)
        scores = jnp.einsum('bhsd,bhtd->bhst', q, k) / scale
        scores = jnp.clip(scores, -50.0, 50.0)
        scores = jnp.nan_to_num(scores, nan=0.0, posinf=50.0, neginf=-50.0)
        attend = (attention_mask.astype(jnp.float32) > 0.5)[:, None, None, :]
        scores = jnp.where(attend, scores, -10000.0)
        scores = jnp.clip(scores, -50.0, 50.0)
        probs = jax.nn.softmax(scores, axis=-1)
        probs = jnp.nan_to_num(probs, nan=0.0, posinf=1.0, neginf=0.0)
        probs = probs / (probs.sum(axis=-1, keepdims=True) + 1e-08)
        ctx = jnp.einsum('bhst,bhtd->bhsd', probs, v)
        ctx = ctx.transpose(0, 2, 1, 3).reshape(B, S, H)
        delta = _nan_clean(ctx @ Wo.T + bo)
        rs = jnp.clip(residual_scale, 0.0, RES_SCALE_MAX)
        delta = rs * delta
        mu = delta.mean(axis=-1, keepdims=True)
        var = jnp.mean((delta - mu) ** 2, axis=-1, keepdims=True)
        delta = (delta - mu) / jnp.sqrt(var + EPS_LN) * ln_gamma + ln_beta
        return delta

    def _L0_ffn_ref(hidden_states, router_w, gate_w, up_w, down_w):
        import jax, jax.numpy as jnp
        import numpy as np
        B, S, H, I, E = (2, 256, 256, 176, 8)
        TOP_K = 2
        b, s, h = hidden_states.shape
        e = router_w.shape[0]
        x = hidden_states.reshape(-1, h)
        logits = jnp.einsum('th,eh->te', x, router_w)
        top_vals, top_idx = jax.lax.top_k(logits, TOP_K)
        top_w = jax.nn.softmax(top_vals, axis=-1)
        expert = top_idx[:, 0]
        weight = top_w[:, 0]
        gate = jnp.einsum('th,eih->eti', x, gate_w)
        up = jnp.einsum('th,eih->eti', x, up_w)
        act = jax.nn.silu(gate) * up
        out_e = jnp.einsum('eti,ehi->eth', act, down_w)
        combine = jax.nn.one_hot(expert, e, dtype=x.dtype) * weight[:, None]
        out = jnp.einsum('eth,te->th', out_e, combine)
        return out.reshape(b, s, h)
    x = x + jnp.tanh(g_xattn[0]) * _L0_xattn_ref(_layernorm(x, axis=-1), ctx_2048, mask_BxS2_ik0, L0_xattn_Wq, L0_xattn_bq, L0_xattn_Wk, L0_xattn_bk, L0_xattn_Wv, L0_xattn_bv, L0_xattn_Wo, L0_xattn_bo, L0_xattn_ln_gamma, L0_xattn_ln_beta, L0_xattn_residual_scale)
    x = x + jnp.tanh(g_ffn[0]) * _L0_ffn_ref(_layernorm(x, axis=-1), L0_ffn_router_w, L0_ffn_gate_w, L0_ffn_up_w, L0_ffn_down_w)
    return x

_drawn_inputs = setup_inputs


def setup_inputs(seed=0):
    import zlib

    import numpy as np

    out = dict(_drawn_inputs(seed))
    spreads = {'L0_xattn_bq': (0.0, 0.1),
     'L0_xattn_bk': (0.0, 0.1),
     'L0_xattn_bv': (0.0, 0.1),
     'L0_xattn_bo': (0.0, 0.1),
     'L0_xattn_ln_gamma': (1.0, 0.2),
     'L0_xattn_ln_beta': (0.0, 0.1)}
    factors = {}
    for name, (base, spread) in spreads.items():
        noise = np.random.default_rng([zlib.crc32(name.encode()), seed]).standard_normal(out[name].shape)
        drawn = base * np.exp(spread * noise) if base else spread * noise
        out[name] = jnp.asarray(drawn.astype(out[name].dtype))
    for name, factor in factors.items():
        out[name] = (out[name] * factor).astype(out[name].dtype)
    return out
```

```python
from contextlib import ExitStack

import numpy as np

import concourse.bass as bass
from concourse import mybir

F32 = mybir.dt.float32
F32R = mybir.dt.float32r
I32 = mybir.dt.int32
ALU = mybir.AluOpType
ACT = mybir.ActivationFunctionType
AX_X = mybir.AxisListType.X

P = 128
B, S, T, D = 32, 100, 1444, 256
H, HD = 16, 16
E, I = 8, 176
EPS_LN = 1e-5
EPS_PROBS = 1e-8
SCORE_CLIP = 50.0
RES_SCALE_MAX = 0.3
EXP_HI = float(np.exp(np.float64(SCORE_CLIP)))
EXP_LO = float(np.exp(np.float64(-SCORE_CLIP)))

KC = D // P
TOK = B * S
NT = TOK // P
BT = 5
NBLK = NT // BT

CPB = 4
CHUNK = T // CPB
CW = CHUNK + 1
KEYS = [121, 120, 120]
KOFF = [0, 121, 241]
NKT = len(KEYS)
G, HG = 4, 4
GR = HG * HD
UPC = 2 * NKT
UPB = UPC * CPB
NCH = B * CPB
NE = 4
LAG = 3
VW = HD + 1

NF = E * I // P


def build(nc, x, ctx_t, mask_t, g_xattn, g_ffn, wq, bq, wk, bk, wv, bv, wo, bo, gamma, beta, rs, router,
          gate, up, down, out):
    top = ExitStack()

    def sem(name):
        return top.enter_context(nc.semaphore(name))

    def sb(stack, name, shape, dt=F32):
        return stack.enter_context(nc.sbuf_tensor(name, shape, dt))

    with top:
        ps = top.enter_context(nc.psum_tensor("ps", [P, 8, 512], F32))
        psf = ps[:].rearrange("p b n -> p (b n)")
        x_all = sb(top, "x_all", [P, NT, D])
        qc = sb(top, "qc", [P, G, TOK])
        ident = sb(top, "ident", [P, P])
        row_of_sum = sb(top, "row_of_sum", [P, P])
        wo_sb = sb(top, "wo_sb", [P, G, D])
        gam = sb(top, "gam", [P, D])
        bet = sb(top, "bet", [P, D])
        bo_sb = sb(top, "bo_sb", [P, D])
        bv_sb = sb(top, "bv_sb", [P, D])
        bq_sb = sb(top, "bq_sb", [P, G])
        bk_sb = sb(top, "bk_sb", [P, KC])
        rw_sb = sb(top, "rw_sb", [P, KC, E])
        scal = sb(top, "scal", [P, 3])
        tg = sb(top, "tg", [P, 2])
        rsc = sb(top, "rsc", [P, 1])
        stats = sb(top, "stats", [P, NT, 6])
        mean = sb(top, "mean", [P, NT])
        var = sb(top, "var", [P, NT])
        tmp_s = sb(top, "tmp_s", [P, 2, NT])
        rstd = sb(top, "rstd", [P, NT])
        eps_ln = sb(top, "eps_ln", [P, 1])
        lg = sb(top, "lg", [P, NT, E])

        params_loaded = sem("params_loaded")
        x_loaded = [sem(f"x_loaded{k}") for k in range(NBLK)]
        consts_made = sem("consts_made")
        chain = sem("chain")
        std_ready = sem("std_ready")
        var_ready = sem("var_ready")

        attn = ExitStack()
        mask_i = sb(attn, "mask_i", [P, NKT, NCH], I32)
        m_scale = sb(attn, "m_scale", [P, NKT, NCH])
        m_bias = sb(attn, "m_bias", [P, NKT, NCH])
        w_raw = sb(attn, "w_raw", [P, KC, D])
        w_raw2 = sb(attn, "w_raw2", [P, KC, D])
        w_raw3 = sb(attn, "w_raw3", [P, KC, D])
        wk_p = sb(attn, "wk_p", [P, 2, KC, D], F32R)
        wv_p = sb(attn, "wv_p", [P, 2, KC, D], F32R)
        head_mask = sb(attn, "head_mask", [P, HG, S])
        zeros = sb(attn, "zeros", [P, 512])

        first = ExitStack()
        wq_p = sb(first, "wq_p", [P, 2, KC, G, 2, GR], F32R)
        hs = sb(first, "hs", [P, BT, D])
        hst_p = sb(first, "hst_p", [P, 2, KC, BT * P], F32R)
        first.close()

        at_raw = sb(attn, "at_raw", [P, 2, KC, CHUNK])
        at_p = sb(attn, "at_p", [P, 2, 2, KC, CW], F32R)
        kt_p = sb(attn, "kt_p", [P, 2, G, CW], F32R)
        v_sb = sb(attn, "v_sb", [P, 2, NKT, H, VW])
        ex = sb(attn, "ex", [P, NE, 2, HG * S])
        qbd = sb(attn, "qbd", [P, 2, 2, G, HG, S], F32R)
        qprod = sb(attn, "qprod", [P, 2, HG, S])
        attn.close()

        ffn = ExitStack()
        outp = ExitStack()
        ctxn = sb(outp, "ctxn", [P, 2, G, P])
        nrm = sb(outp, "nrm", [P, 3, G * P])
        outp.close()
        actt_p = sb(ffn, "actt_p", [P, 2, NF, P], F32R)
        tgg = sb(ffn, "tgg", [P, D])
        tgb = sb(ffn, "tgb", [P, D])
        yv = sb(ffn, "yv", [P, 2, D])
        xn = sb(ffn, "xn", [P, 2, D])
        xts = sb(ffn, "xts", [P, 2, KC, P])
        w_stage = sb(ffn, "w_stage", [P, 2, 4 * I])
        gu_p = sb(ffn, "gu_p", [P, 2, KC, E, 2 * I], F32R)
        dn_p = sb(ffn, "dn_p", [P, 2, NF, D], F32R)
        xs_p = sb(ffn, "xs_p", [P, 2, 2, KC, P], F32R)
        sil = sb(ffn, "sil", [P, 3, I])
        act = sb(ffn, "act", [P, 2, NF * P])
        y_out = sb(ffn, "y_out", [P, 2, D])
        r_a = sb(ffn, "r_a", [P, NT, E])
        r_b = sb(ffn, "r_b", [P, NT, E])
        iota_e = sb(ffn, "iota_e", [P, NT, E])
        r_m = sb(ffn, "r_m", [P, 4, NT])
        ffn.close()

        hs_ready = sem("hs_ready")
        hs_transposed = sem("hs_transposed")
        hst_hi = sem("hst_hi")
        hst_lo = sem("hst_lo")
        wq_split = sem("wq_split")
        q_projected = sem("q_projected")
        q_stored = sem("q_stored")
        w_split = sem("w_split")
        mask_ready = sem("mask_ready")
        pads_set = sem("pads_set")
        at_loaded = [sem("at_loaded0"), sem("at_loaded1")]
        at_split = sem("at_split")
        k_projected = sem("k_projected")
        k_hi = sem("k_hi")
        k_lo = sem("k_lo")
        v_projected = sem("v_projected")
        v_ready = sem("v_ready")
        q_built = sem("q_built")
        pool_chain = sem("pool_chain")
        scored = sem("scored")
        exped = sem("exped")
        clipped = sem("clipped")
        pv_done = sem("pv_done")
        ctx_cleared = sem("ctx_cleared")
        ctx_saved = sem("ctx_saved")
        sums_spread = sem("sums_spread")
        sums_copied = sem("sums_copied")
        ctx_normed = sem("ctx_normed")
        o_projected = sem("o_projected")
        delta_ready = sem("delta_ready")
        gates_ready = sem("gates_ready")
        xn_ready = sem("xn_ready")
        xn_transposed = sem("xn_transposed")
        xts_ready = sem("xts_ready")
        xt_kept = sem("xt_kept")
        logits_done = sem("logits_done")
        logits_kept = sem("logits_kept")
        gap_ready = sem("gap_ready")
        gap_exped = sem("gap_exped")
        combine_ready = sem("combine_ready")
        stage_loaded = [sem("stage_loaded0"), sem("stage_loaded1")]
        stage_split = sem("stage_split")
        xs_hi = sem("xs_hi")
        xs_lo = sem("xs_lo")
        gu_done = sem("gu_done")
        silu_done = sem("silu_done")
        act_ready = sem("act_ready")
        act_transposed = sem("act_transposed")
        actt_hi = sem("actt_hi")
        actt_lo = sem("actt_lo")
        down_done = sem("down_done")
        y_ready = sem("y_ready")
        y_stored = [sem("y_stored0"), sem("y_stored1")]

        def tps(kc, lo, n):
            return psf[:, kc * 1024 + lo:kc * 1024 + lo + n]

        def qps(g, half):
            return ps[:, 4 + 2 * (g % 2) + half, 0:BT * P // 2]

        def kps(m):
            return ps[:, m, 0:CW]
        vps = ps[:, 2, 0:D]
        ctx_ps = ps[:, 3, 0:G * S]

        def sps(u):
            return ps[:, 4 + 2 * (u % 2):6 + 2 * (u % 2), 0:HG * S]

        def used(eng, semaphore, value):
            if not isinstance(value, int) or value > 0:
                eng.wait_ge(semaphore, value)

        block = top.enter_context(nc.Block())

        pieces = []
        for kc in range(KC):
            for e0 in range(0, E, 4):
                pieces.append((lambda p, kc=kc, e0=e0: gu_p[:, p, kc, e0:e0 + 4, 0:I], gate[:, kc, e0:e0 + 4, :], 4, I))
                pieces.append((lambda p, kc=kc, e0=e0: gu_p[:, p, kc, e0:e0 + 4, I:2 * I], up[:, kc, e0:e0 + 4, :], 4, I))
        for f0 in range(0, NF, 2):
            n = min(2, NF - f0)
            pieces.append((lambda p, f0=f0, n=n: dn_p[:, p, f0:f0 + n, :], down[:, f0:f0 + n, :], n, D))

        def stage(k):
            _, _, a, b_ = pieces[k]
            return w_stage[:, k % 2, 0:a * b_].rearrange("p (a b) -> p a b", a=a)

        @block.sync
        def _(sp):
            for k in range(NBLK):
                sp.dma_start(x_all[:, k * BT:(k + 1) * BT, :],
                             x.rearrange("(n p) d -> p n d", p=P)[:, k * BT:(k + 1) * BT, :]).then_inc(x_loaded[k], 16)
            plain = [(w_raw, wq), (w_raw2, wk), (w_raw3, wv), (bq_sb, bq), (bk_sb, bk), (rw_sb, router)]
            for dst, src in plain:
                sp.dma_start(dst[:], src).then_inc(params_loaded, 16)
            for dst, src in ((bv_sb, bv), (bo_sb, bo), (gam, gamma), (bet, beta)):
                sp.dma_start(dst[:], src.partition_broadcast(P)).then_inc(params_loaded, 16)
            for k, src in enumerate((g_xattn, g_ffn, rs)):
                sp.dma_start(scal[:, k:k + 1], src.partition_broadcast(P)).then_inc(params_loaded, 16)
            for t in range(NKT):
                sp.dma_start(mask_i[0:KEYS[t], t, :], mask_t[KOFF[t]:KOFF[t] + KEYS[t], :]).then_inc(params_loaded, 16)
            sp.wait_ge(consts_made, 3)
            for j in range(4):
                sp.dma_start(wo_sb[32 * j:32 * j + HD, :, :], wo[j]).then_inc(params_loaded, 16)

            def load_chunk(b, c):
                sp.dma_start(at_raw[:, c % 2], ctx_t[b * CPB + c] if isinstance(b, int)
                             else ctx_t[bass.ds(b * CPB + c, 1)].rearrange("o p k n -> (o p) k n")
                             ).then_inc(at_loaded[c % 2], 16)
            sp.wait_ge(q_stored, G * NBLK)
            for c in range(CPB):
                if c >= 2:
                    sp.wait_ge(at_split, 2 * (c - 1))
                load_chunk(0, c)
            with sp.Fori(1, B) as b:
                for c in range(CPB):
                    sp.wait_ge(at_split, b * 2 * CPB + 2 * (c - 1))
                    load_chunk(b, c)
            sp.wait_ge(ctx_saved, B)
            for k in range(len(pieces)):
                if k >= 2:
                    sp.wait_ge(stage_split, 2 * (k - 1))
                sp.dma_start(stage(k), pieces[k][1]).then_inc(stage_loaded[k % 2], 16)

            def store(i, slot):
                sp.wait_ge(y_ready, i + 1)
                dst = out[i * P:(i + 1) * P, :] if isinstance(i, int) else out[bass.ds(i * P, P), :]
                sp.dma_start(dst, y_out[:, slot, :]).then_inc(y_stored[slot], 16)
            with sp.Fori(0, NT // 2) as r:
                store(r * 2, 0)
                store(r * 2 + 1, 1)
            store(NT - 1, 0)
            sp.wait_ge(y_stored[0], 16 * (NT // 2 + 1))
            sp.wait_ge(y_stored[1], 16 * (NT // 2))

        @block.gpsimd
        def _(pool):
            nc.gpsimd.memset(ident[:], 1.0).then_inc(pool_chain, 1)
            nc.gpsimd.memset(row_of_sum[:], 1.0).then_inc(pool_chain, 1)
            nc.gpsimd.memset(head_mask[:], 1.0).then_inc(pool_chain, 1)
            pool.wait_ge(pool_chain, 3)
            nc.gpsimd.affine_select(out=ident[:], in_=ident[:], compare_op=ALU.is_equal, fill=0.0, base=0,
                                    pattern=[[-1, P]], channel_multiplier=1).then_inc(consts_made, 1)
            v = row_of_sum[:].rearrange("p (q c) -> p q c", q=4)
            nc.gpsimd.affine_select(out=v, in_=v, compare_op=ALU.is_equal, fill=0.0, base=-HD,
                                    pattern=[[-32, 4], [0, 32]], channel_multiplier=1).then_inc(consts_made, 1)
            nc.gpsimd.memset(wo_sb[:], 0.0).then_inc(consts_made, 1)
            for half in range(2):
                w = head_mask[half * GR:(half + 1) * GR]
                nc.gpsimd.affine_select(out=w, in_=w, compare_op=ALU.is_ge, fill=0.0, base=0,
                                        pattern=[[-HD, HG], [0, S]], channel_multiplier=1).then_inc(pool_chain, 1)
                pool.wait_ge(pool_chain, 4 + 2 * half)
                nc.gpsimd.affine_select(out=w, in_=w, compare_op=ALU.is_ge, fill=0.0, base=HD - 1,
                                        pattern=[[HD, HG], [0, S]], channel_multiplier=-1).then_inc(pool_chain, 1)
            pool.wait_ge(pool_chain, 7)
            BASE = 7

            def build_q(b, slot):
                for g in range(G):
                    k = b * (2 * G) + BASE + 2 * g
                    q = qc[:, g, b * S:(b + 1) * S] if isinstance(b, int) else qc[:, g, bass.ds(b * S, S)]
                    hi = qbd[:, slot, 0, g] if isinstance(b, int) else \
                        qbd[:, bass.ds(slot, 1), 0, g].rearrange("p o h s -> p (o h) s")
                    lo = qbd[:, slot, 1, g] if isinstance(b, int) else \
                        qbd[:, bass.ds(slot, 1), 1, g].rearrange("p o h s -> p (o h) s")
                    prod = qprod[:, g % 2]
                    nc.gpsimd.tensor_tensor(prod, q.unsqueeze(1).to_broadcast([P, HG, S]), head_mask[:],
                                            ALU.mult).then_inc(pool_chain, 1)
                    pool.wait_ge(pool_chain, k + 1)
                    nc.gpsimd.tensor_copy(hi, prod).then_inc(pool_chain, 1)
                    pool.wait_ge(pool_chain, k + 2)
                    nc.gpsimd.tensor_tensor(lo, prod, hi.bitcast(F32), ALU.subtract).then_inc(q_built, 1)

            pool.wait_ge(q_stored, G * NBLK)
            build_q(0, 0)
            build_q(1, 1)
            with pool.Fori(2, B) as b:
                pool.wait_ge(scored, b * UPB - UPB)
                build_q(b, b % 2)

        @block.vector
        def _(dve):
            n_chain = [0]

            def linked(ins):
                n_chain[0] += 1
                ins.then_inc(chain, 1)
                dve.wait_ge(chain, n_chain[0])

            def mean_and_var():
                linked(dve.tensor_tensor(mean[:], stats[:, :, 1], stats[:, :, 4], ALU.add))
                linked(dve.tensor_scalar(mean[:], mean[:], 0.5, None, ALU.mult))
                linked(dve.tensor_tensor(tmp_s[:, 0], stats[:, :, 1], stats[:, :, 4], ALU.subtract))
                linked(dve.scalar_tensor_tensor(out=tmp_s[:, 1], in0=tmp_s[:, 0], scalar=0.25, in1=tmp_s[:, 0],
                                                op0=ALU.mult, op1=ALU.mult))
                linked(dve.tensor_tensor(tmp_s[:, 0], stats[:, :, 2], stats[:, :, 5], ALU.add))
                dve.scalar_tensor_tensor(out=var[:], in0=tmp_s[:, 0], scalar=1.0 / D, in1=tmp_s[:, 1],
                                         op0=ALU.mult, op1=ALU.add).then_inc(var_ready, 1)

            dve.memset(eps_ln[:], EPS_LN).then_inc(var_ready, 1)
            dve.memset(zeros[:], 0.0).then_inc(pads_set, 1)
            for k in range(NBLK):
                dve.wait_ge(x_loaded[k], 16)
                for j in range(BT):
                    n = k * BT + j
                    last = dve.bn_stats(stats[:, n, :], x_all[:, n, :])
            linked(last)
            mean_and_var()
            dve.wait_ge(params_loaded, 16 * 20)
            raw_g = w_raw[:].rearrange("p k (g c) -> p k g c", g=G)
            for twin in range(2):
                dve.tensor_copy(wq_p[:, 0, :, :, twin, :], raw_g).then_inc(wq_split, 1)
            dve.wait_ge(wq_split, 2)
            for twin in range(2):
                for kc in range(KC):
                    dve.tensor_tensor(wq_p[:, 1, kc, :, twin, :], raw_g[:, kc], wq_p[:, 0, kc, :, twin, :].bitcast(F32),
                                      ALU.subtract).then_inc(wq_split, 1)
            dve.tensor_copy(wk_p[:, 0], w_raw2[:]).then_inc(w_split, 1)
            dve.tensor_copy(wv_p[:, 0], w_raw3[:]).then_inc(w_split, 1)
            dve.wait_ge(w_split, 2)
            dve.tensor_tensor(wk_p[:, 1], w_raw2[:], wk_p[:, 0].bitcast(F32), ALU.subtract).then_inc(w_split, 1)
            dve.tensor_tensor(wv_p[:, 1], w_raw3[:], wv_p[:, 0].bitcast(F32), ALU.subtract).then_inc(w_split, 1)
            inv = 1.0 / float(np.sqrt(HD))
            for t in range(NKT):
                linked(dve.tensor_scalar(m_scale[0:KEYS[t], t], mask_i[0:KEYS[t], t], 0.5, inv, ALU.is_gt, ALU.mult))
                dve.tensor_scalar(m_bias[0:KEYS[t], t], m_scale[0:KEYS[t], t], SCORE_CLIP / inv, -SCORE_CLIP,
                                  ALU.mult, ALU.add).then_inc(mask_ready, 1)
            dve.wait_ge(std_ready, 1)
            linked(dve.reciprocal(rstd[:], rstd[:]))
            for k in range(NBLK):
                for j in range(BT):
                    n = k * BT + j
                    if k >= 1:
                        dve.wait_ge(hs_transposed, k)
                    dve.tensor_scalar(hs[:, j, :], x_all[:, n, :], mean[:, n:n + 1], rstd[:, n:n + 1],
                                      ALU.subtract, ALU.mult).then_inc(hs_ready, 1)
                for kc in range(KC):
                    dve.wait_ge(hst_hi, KC * k + kc + 1)
                    dve.tensor_tensor(hst_p[:, 1, kc], tps(kc, 0, BT * P), hst_p[:, 0, kc].bitcast(F32),
                                      ALU.subtract).then_inc(hst_lo, 1)

            dve.wait_ge(q_stored, G * NBLK)
            dve.memset(v_sb[:, :, :, :, HD:VW], 1.0).then_inc(pads_set, 1)
            dve.memset(at_p[:, :, :, :, CHUNK:CW].bitcast(F32), 0.0).then_inc(pads_set, 1)

            def split_hi(g, c):
                s = c % 2
                dve.wait_ge(at_loaded[s], (g - s) * 8 + 16)
                if not (isinstance(g, int) and g < 2):
                    dve.wait_ge(v_projected, NKT * (g - 1))
                dve.tensor_copy(at_p[:, s, 0, :, 0:CHUNK], at_raw[:, s]).then_inc(at_split, 1)

            def split_lo(g, c):
                s = c % 2
                dve.wait_ge(at_split, g * 2 + 1)
                dve.tensor_tensor(at_p[:, s, 1, :, 0:CHUNK], at_raw[:, s], at_p[:, s, 0, :, 0:CHUNK].bitcast(F32),
                                  ALU.subtract).then_inc(at_split, 1)

            def key_lo(g, c, m):
                for h in range(2):
                    grp = 2 * m + h
                    dve.wait_ge(k_hi, g * G + grp + 1)
                    dve.scalar_tensor_tensor(out=kt_p[GR:P, c % 2, grp, :], in0=kps(m)[h * GR:(h + 1) * GR],
                                             scalar=bk_sb[h * GR:(h + 1) * GR, m:m + 1],
                                             in1=kt_p[0:GR, c % 2, grp, :].bitcast(F32),
                                             op0=ALU.add, op1=ALU.subtract).then_inc(k_lo, 1)

            def value_tile(g, c, t):
                dve.wait_ge(v_projected, g * NKT + t + 1)
                if not (isinstance(g, int) and g < 2):
                    dve.wait_ge(pv_done, (g - 2) * UPC + 2 * t + 2)
                n = KEYS[t]
                dve.tensor_tensor(v_sb[0:n, c % 2, t, :, 0:HD], vps[0:n].rearrange("p (h d) -> p h d", h=H),
                                  bv_sb[0:n].rearrange("p (h d) -> p h d", h=H), ALU.add).then_inc(v_ready, 1)

            def clip(U, u):
                dve.wait_ge(exped, U + 1)
                n = KEYS[(u % UPC) // 2]
                e = ex[0:n, u % NE]
                dve.tensor_scalar(e, e, EXP_LO, EXP_HI, ALU.max, ALU.min).then_inc(clipped, 1)

            def attend(b, last_batch):
                for u in range(UPB):
                    c, v = divmod(u, UPC)
                    g = b * CPB + c
                    more = not (last_batch and c == CPB - 1)
                    if v in (2, 5) and more:
                        value_tile(g + 1, c + 1, 0 if v == 2 else 2)
                    clip(b * UPB + u, u)
                    if v == 3 and more:
                        value_tile(g + 1, c + 1, 1)
                    if v < 2 and more:
                        key_lo(g + 1, c + 1, v)
                    if not (last_batch and c >= CPB - 2):
                        if v == 2:
                            split_hi(g + 2, c)
                        if v == 4:
                            split_lo(g + 2, c)
            for g in range(2):
                split_hi(g, g)
                split_lo(g, g)
            key_lo(0, 0, 0)
            key_lo(0, 0, 1)
            for t in range(NKT):
                value_tile(0, 0, t)
            attend(0, False)
            with dve.Fori(1, B - 1) as b:
                attend(b, False)
            attend(B - 1, True)

            dve.wait_ge(ctx_saved, B)
            dve.wait_ge(gates_ready, 2)
            linked(dve.tensor_scalar(rsc[:], scal[:, 2:3], 0.0, RES_SCALE_MAX, ALU.max, ALU.min))
            linked(dve.tensor_scalar(bo_sb[:], bo_sb[:], rsc[:, 0:1], None, ALU.mult))
            dve.tensor_scalar(tgg[:], gam[:], tg[:, 0:1], None, ALU.mult)
            dve.tensor_scalar(tgb[:], bet[:], tg[:, 0:1], None, ALU.mult)
            C2 = n_chain[0]

            def tile_cols(ap, i):
                return ap[:, :, i * P:(i + 1) * P] if isinstance(i, int) else ap[:, :, bass.ds(i * P, P)]

            def one(ap, i):
                return ap[:, i] if isinstance(i, int) else ap[:, bass.ds(i, 1)].rearrange("p o n -> p (o n)")

            LINKS = 3
            def output_block(k):
                for j in range(BT):
                    i = k * BT + j
                    base = i * LINKS + C2
                    dve.wait_ge(sums_copied, i + 1)
                    dve.scalar_tensor_tensor(out=nrm[:, 1], in0=nrm[:, 0], scalar=EPS_PROBS, in1=nrm[:, 0],
                                             op0=ALU.mult, op1=ALU.add).then_inc(chain, 1)
                    dve.wait_ge(chain, base + 1)
                    dve.reciprocal(nrm[:, 2], nrm[:, 1]).then_inc(chain, 1)
                    dve.wait_ge(chain, base + 2)
                    used(dve, o_projected, i if j == 0 else i - 1)
                    dve.tensor_tensor(ctxn[:, j % 2], tile_cols(qc, i), nrm[:, 2].rearrange("p (g s) -> p g s", g=G),
                                      ALU.mult).then_inc(ctx_normed, 1)
                    dve.wait_ge(o_projected, i + 1)
                    d = tile_cols(qc[:, 0:2], i)
                    dve.scalar_tensor_tensor(out=d, in0=ps[:, 2 + j % 2, 0:D].rearrange("p (k n) -> p k n", k=2),
                                             scalar=rsc[:, 0:1], in1=bo_sb[:].rearrange("p (k n) -> p k n", k=2),
                                             op0=ALU.mult, op1=ALU.add).then_inc(chain, 1)
                    dve.wait_ge(chain, base + 3)
                    dve.bn_stats(one(stats, i), d).then_inc(delta_ready, 1)
            output_block(0)
            with dve.Fori(1, NBLK) as k:
                output_block(k)
            n_chain[0] = C2 + LINKS * NT
            dve.wait_ge(delta_ready, NT)
            mean_and_var()
            dve.wait_ge(std_ready, 2)
            linked(dve.reciprocal(rstd[:], rstd[:]))
            for i in range(NT):
                d = tile_cols(qc[:, 0:2], i)
                y = yv[:, i % 2]
                linked(dve.tensor_scalar(y.rearrange("p (k n) -> p k n", k=2), d, mean[:, i:i + 1], rstd[:, i:i + 1],
                                         ALU.subtract, ALU.mult))
                linked(dve.tensor_tensor(y, y, tgg[:], ALU.mult))
                linked(dve.tensor_tensor(y, y, tgb[:], ALU.add))
                linked(dve.tensor_tensor(x_all[:, i], x_all[:, i], y, ALU.add))
                linked(dve.bn_stats(stats[:, i, :], x_all[:, i]))
            mean_and_var()
            dve.wait_ge(std_ready, 3)
            linked(dve.reciprocal(rstd[:], rstd[:]))

            for i in range(NT):
                if i >= 2:
                    dve.wait_ge(xn_transposed, i - 1)
                dve.tensor_scalar(xn[:, i % 2], x_all[:, i], mean[:, i:i + 1], rstd[:, i:i + 1],
                                  ALU.subtract, ALU.mult).then_inc(xn_ready, 1)
                if i >= 1:
                    dve.wait_ge(logits_done, i)
                    dve.tensor_copy(lg[:, i - 1], ps[:, 2 + (i - 1) % 2, 0:E]).then_inc(logits_kept, 1)
            dve.wait_ge(logits_done, NT)
            dve.tensor_copy(lg[:, NT - 1], ps[:, 2 + (NT - 1) % 2, 0:E]).then_inc(logits_kept, 1)
            dve.wait_ge(logits_kept, NT)
            for e in range(E):
                dve.memset(iota_e[:, :, e:e + 1], float(e))
            m1, m2, first_e, wgt = (r_m[:, q] for q in range(4))

            def wide(m):
                return m.unsqueeze(2).to_broadcast([P, NT, E])
            linked(dve.tensor_reduce(m1, lg[:], AX_X, ALU.max))
            linked(dve.tensor_tensor(r_a[:], lg[:], wide(m1), ALU.not_equal))
            linked(dve.scalar_tensor_tensor(out=r_b[:], in0=r_a[:], scalar=float(E), in1=iota_e[:], op0=ALU.mult,
                                            op1=ALU.add))
            linked(dve.tensor_reduce(first_e, r_b[:], AX_X, ALU.min))
            linked(dve.tensor_tensor(r_a[:], iota_e[:], wide(first_e), ALU.is_equal))
            linked(dve.scalar_tensor_tensor(out=r_b[:], in0=r_a[:], scalar=-3.0e38, in1=lg[:], op0=ALU.mult,
                                            op1=ALU.add))
            linked(dve.tensor_reduce(m2, r_b[:], AX_X, ALU.max))
            linked(dve.tensor_tensor(first_e, m2, m1, ALU.subtract))
            dve.tensor_copy(m2, first_e).then_inc(gap_ready, 1)
            dve.wait_ge(gap_exped, 1)
            linked(dve.tensor_scalar(wgt, wgt, 1.0, None, ALU.add))
            linked(dve.reciprocal(wgt, wgt))
            dve.tensor_tensor(lg[:], r_a[:], wide(wgt), ALU.mult).then_inc(combine_ready, 1)

            for k, (dst, _, _, _) in enumerate(pieces):
                dve.wait_ge(stage_loaded[k % 2], 16 * (k // 2 + 1))
                dve.tensor_copy(dst(0), stage(k)).then_inc(stage_split, 1)
                dve.wait_ge(stage_split, 2 * k + 1)
                dve.tensor_tensor(dst(1), stage(k), dst(0).bitcast(F32), ALU.subtract).then_inc(stage_split, 1)
            dve.wait_ge(combine_ready, 1)

            def input_lo(i, slot):
                dve.wait_ge(xs_hi, i + 1)
                dve.tensor_tensor(xs_p[:, slot, 1], tile_cols(qc[:, 2:4], i), xs_p[:, slot, 0].bitcast(F32),
                                  ALU.subtract).then_inc(xs_lo, 1)

            def hidden(i, slot, e):
                dve.wait_ge(silu_done, i * E + e + 1)
                n = (slot * E + e) % 2
                col = lg[:, i, e:e + 1] if isinstance(i, int) else \
                    lg[:, bass.ds(i, 1), e:e + 1].rearrange("p o n -> p (o n)")
                dve.scalar_tensor_tensor(out=act[:, slot, e * I:(e + 1) * I], in0=sil[:, e % 2], scalar=col,
                                         in1=ps[:, n, I:2 * I], op0=ALU.mult, op1=ALU.mult).then_inc(act_ready, 1)

            def hidden_lo(i, q):
                n = min(4, NF - 4 * q)
                dve.wait_ge(actt_hi, i * 3 + q + 1)
                dve.tensor_tensor(actt_p[:, 1, 4 * q:4 * q + n].rearrange("p f n -> p (f n)"), ps[:, 2 + q, 0:n * P],
                                  actt_p[:, 0, 4 * q:4 * q + n].rearrange("p f n -> p (f n)").bitcast(F32),
                                  ALU.subtract).then_inc(actt_lo, 1)

            def finish(i, slot):
                dve.wait_ge(down_done, i + 1)
                if isinstance(i, int):
                    if i >= 2:
                        dve.wait_ge(y_stored[slot], 16 * (i // 2))
                else:
                    dve.wait_ge(y_stored[slot], (i - slot) * 8)
                dve.scalar_tensor_tensor(out=y_out[:, slot], in0=ps[:, 5, 0:D], scalar=tg[:, 1:2], in1=one(x_all, i),
                                         op0=ALU.mult, op1=ALU.add).then_inc(y_ready, 1)

            def expert_tile(i, slot, has_before, has_next):
                if has_next:
                    input_lo(i + 1, 1 - slot)
                for e in range(E):
                    hidden(i, slot, e)
                    if has_before:
                        if 2 <= e < 5:
                            hidden_lo(i - 1, e - 2)
                        if e == 7:
                            finish(i - 1, 1 - slot)
            input_lo(0, 0)
            expert_tile(0, 0, False, True)
            expert_tile(1, 1, True, True)
            with dve.Fori(1, NT // 2) as r:
                expert_tile(r * 2, 0, True, True)
                expert_tile(r * 2 + 1, 1, True, True)
            expert_tile(NT - 1, 0, True, False)
            for q in range(3):
                hidden_lo(NT - 1, q)
            finish(NT - 1, 0)

        @block.scalar
        def _(ac):
            def roots(k):
                ac.wait_ge(var_ready, k + 2)
                ac.activation(rstd[:], var[:], ACT.Sqrt, bias=eps_ln[:, 0:1]).then_inc(std_ready, 1)

            roots(0)
            ac.wait_ge(params_loaded, 16 * 20)
            for k in range(NBLK):
                for kc in range(KC):
                    ac.wait_ge(hs_transposed, k + 1)
                    if k >= 1:
                        ac.wait_ge(q_projected, G * k)
                    ac.copy(hst_p[:, 0, kc], tps(kc, 0, BT * P)).then_inc(hst_hi, 1)
                for g in range(G):
                    ac.wait_ge(q_projected, G * k + g + 1)
                    ac.activation(qc[:, g, k * BT * P:(k + 1) * BT * P].rearrange("p (h n) -> p h n", h=2),
                                  ps[:, 4 + 2 * (g % 2):6 + 2 * (g % 2), 0:BT * P // 2], ACT.Identity,
                                  bias=bq_sb[:, g:g + 1]).then_inc(q_stored, 1)

            ac.wait_ge(mask_ready, NKT)
            ac.wait_ge(q_stored, G * NBLK)

            def key_hi(g, c, m):
                ac.wait_ge(k_projected, g * 2 + m + 1)
                if not (isinstance(g, int) and g < 2):
                    ac.wait_ge(scored, g * UPC - UPC)
                for h in range(2):
                    ac.activation(kt_p[0:GR, c % 2, 2 * m + h, :], kps(m)[h * GR:(h + 1) * GR], ACT.Identity,
                                  bias=bk_sb[h * GR:(h + 1) * GR, m:m + 1]).then_inc(k_hi, 1)

            def column(tab, n, t, g):
                return tab[0:n, t, g:g + 1] if isinstance(g, int) else tab[0:n, t, bass.ds(g, 1)]

            def expo(b, u, g):
                n, t = KEYS[(u % UPC) // 2], (u % UPC) // 2
                U = b * UPB + u
                ac.wait_ge(scored, U + 1)
                if not (isinstance(b, int) and b * UPB + u < NE):
                    ac.wait_ge(pv_done, U - (NE - 1))
                ac.nop(nofuse=True)
                ac.activation(ex[0:n, u % NE], sps(u)[0:n], ACT.Exp, bias=column(m_bias, n, t, g),
                              scale=column(m_scale, n, t, g)).then_inc(exped, 1)

            def save_ctx(b):
                ac.wait_ge(pv_done, b * UPB + UPB)
                ac.wait_ge(q_built, b * G + G)
                dst = qc[:, :, b * S:(b + 1) * S] if isinstance(b, int) else qc[:, :, bass.ds(b * S, S)]
                ac.copy(dst, ctx_ps.rearrange("p (g s) -> p g s", g=G)).then_inc(ctx_saved, 1)

            def attend(b, first_batch, last_batch):
                for u in range(UPB):
                    c, v = divmod(u, UPC)
                    g = b * CPB + c
                    expo(b, u, g)
                    if v < 2 and not (last_batch and c == CPB - 1):
                        key_hi(g + 1, c + 1, v)
                    if u == LAG - 1 and not first_batch:
                        save_ctx(b - 1)
            key_hi(0, 0, 0)
            key_hi(0, 0, 1)
            attend(0, True, False)
            with ac.Fori(1, B - 1) as b:
                attend(b, False, False)
            attend(B - 1, False, True)
            save_ctx(B - 1)

            ac.activation(tg[:, 0:1], scal[:, 0:1], ACT.Tanh).then_inc(gates_ready, 1)
            ac.activation(tg[:, 1:2], scal[:, 1:2], ACT.Tanh).then_inc(gates_ready, 1)
            def copy_sums(k):
                for j in range(BT):
                    i = k * BT + j
                    ac.wait_ge(sums_spread, i + 1)
                    used(ac, ctx_normed, i)
                    ac.copy(nrm[:, 0], ps[:, j % 2]).then_inc(sums_copied, 1)
            copy_sums(0)
            with ac.Fori(1, NBLK) as k:
                copy_sums(k)
            roots(1)
            roots(2)

            for i in range(NT):
                ac.wait_ge(xn_transposed, i + 1)
                if i >= 2:
                    ac.wait_ge(logits_done, i - 1)
                src = ps[:, i % 2, 0:D].rearrange("p (k n) -> p k n", k=KC)
                ac.copy(xts[:, i % 2], src).then_inc(xts_ready, 1)
                ac.copy(qc[:, 2:4, i * P:(i + 1) * P], src).then_inc(xt_kept, 1)
            ac.wait_ge(gap_ready, 1)
            ac.activation(r_m[:, 3], r_m[:, 1], ACT.Exp).then_inc(gap_exped, 1)

            ac.wait_ge(xt_kept, NT)

            def input_hi(i, slot):
                if not (isinstance(i, int) and i < 2):
                    ac.wait_ge(gu_done, i * E - E)
                src = qc[:, 2:4, i * P:(i + 1) * P] if isinstance(i, int) else qc[:, 2:4, bass.ds(i * P, P)]
                ac.copy(xs_p[:, slot, 0], src).then_inc(xs_hi, 1)

            def silu(i, slot, e):
                ac.wait_ge(gu_done, i * E + e + 1)
                if not (isinstance(i, int) and i == 0 and e < 2):
                    ac.wait_ge(act_ready, i * E + e - 1)
                ac.activation(sil[:, e % 2], ps[:, e % 2, 0:I], ACT.Silu).then_inc(silu_done, 1)

            def hidden_hi(i, q):
                n = min(4, NF - 4 * q)
                ac.wait_ge(act_transposed, i * 3 + q + 1)
                if not (isinstance(i, int) and i == 0):
                    ac.wait_ge(down_done, i)
                ac.copy(actt_p[:, 0, 4 * q:4 * q + n].rearrange("p f n -> p (f n)"), ps[:, 2 + q, 0:n * P]
                        ).then_inc(actt_hi, 1)

            def expert_tile(i, slot, has_before, has_next):
                if has_next:
                    input_hi(i + 1, 1 - slot)
                for e in range(E):
                    silu(i, slot, e)
                    if has_before and 2 <= e < 5:
                        hidden_hi(i - 1, e - 2)
            input_hi(0, 0)
            expert_tile(0, 0, False, True)
            expert_tile(1, 1, True, True)
            with ac.Fori(1, NT // 2) as r:
                expert_tile(r * 2, 0, True, True)
                expert_tile(r * 2 + 1, 1, True, True)
            expert_tile(NT - 1, 0, True, False)
            for q in range(3):
                hidden_hi(NT - 1, q)

        @block.tensor
        def _(pe):
            def parts(dst, lhs, rhs, rounds):
                last = None
                todo = [(k, a, b) for k in range(rounds) for a, b in ((0, 0), (0, 1), (1, 0))]
                for q, (k, a, b) in enumerate(todo):
                    last = pe.matmul(dst, lhs(a, k), rhs(b, k), start=q == 0, stop=q == len(todo) - 1)
                return last

            pe.wait_ge(consts_made, 1)
            for k in range(NBLK):
                if k >= 1:
                    pe.wait_ge(hst_lo, KC * k)
                for j in range(BT):
                    pe.wait_ge(hs_ready, BT * k + j + 1)
                    for kc in range(KC):
                        last = pe.transpose(tps(kc, j * P, P), hs[:, j, kc * P:(kc + 1) * P], ident[:])
                last.then_inc(hs_transposed, 1)
                pe.wait_ge(hst_lo, KC * (k + 1))
                pe.wait_ge(wq_split, 2 + 2 * KC)
                for g in range(G):
                    n = G * k + g
                    if n >= 2:
                        pe.wait_ge(q_stored, n - 1)
                    for half in range(2):
                        w = BT * P // 2
                        last = parts(qps(g, half),
                                     lambda p, kc: wq_p[:, p, kc, g].rearrange("p t c -> p (t c)"),
                                     lambda p, kc: hst_p[:, p, kc, half * w:(half + 1) * w], KC)
                    last.then_inc(q_projected, 1)

            pe.wait_ge(w_split, 4)
            pe.wait_ge(pads_set, 3)
            pe.wait_ge(q_stored, G * NBLK)
            pe.matmul(ps[:, 3, :], zeros[:, 0:P], zeros[:], start=True, stop=True).then_inc(ctx_cleared, 1)

            def project_keys(g, c, m):
                pe.wait_ge(at_split, g * 2 + 2)
                if not (isinstance(g, int) and g < 1):
                    pe.wait_ge(k_lo, g * G - G + 2 * m + 2)
                s = c % 2
                parts(kps(m), lambda p, kc: wk_p[:, p, kc, m * P:(m + 1) * P], lambda p, kc: at_p[:, s, p, kc, :],
                      KC).then_inc(k_projected, 1)

            def project_values(g, c, t):
                if not (isinstance(g, int) and g * NKT + t < 1):
                    pe.wait_ge(v_ready, g * NKT + t)
                s, o, n = c % 2, KOFF[t], KEYS[t]
                parts(vps[0:n], lambda p, kc: at_p[:, s, p, kc, o:o + n], lambda p, kc: wv_p[:, p, kc, :],
                      KC).then_inc(v_projected, 1)

            def scores(b, u, g):
                v = u % UPC
                t, half = v // 2, v % 2
                o, n = KOFF[t], KEYS[t]
                U = b * UPB + u
                if not (isinstance(b, int) and b == 0 and u < 2):
                    pe.wait_ge(exped, U - 1)
                if t == 0:
                    pe.wait_ge(k_lo, g * G + 2 * half + 2)
                if u == 0:
                    pe.wait_ge(q_built, b * G + G)
                last = None
                for h in range(2):
                    grp = 2 * half + h
                    for part in range(2):
                        q = qbd[:, b % 2, part, grp] if isinstance(b, int) else \
                            qbd[:, bass.ds(b % 2, 1), part, grp].rearrange("p o h s -> p (o h) s")
                        last = pe.matmul(sps(u)[0:n, h], kt_p[:, (u // UPC) % 2, grp, o:o + n],
                                         q, start=part == 0, stop=part == 1)
                last.then_inc(scored, 1)

            def weigh_values(b, u):
                v = u % UPC
                c, t, half = u // UPC, v // 2, v % 2
                n = KEYS[t]
                U = b * UPB + u
                pe.wait_ge(clipped, U + 1)
                if half == 0:
                    pe.wait_ge(v_ready, (b * CPB + c) * NKT + t + 1)
                if u == 0 and not (isinstance(b, int) and b == 0):
                    pe.wait_ge(ctx_saved, b)
                last = None
                for q in range(2 * HG):
                    h = 2 * HG * half + q
                    s, j = h // HG, h % HG
                    last = pe.matmul(ctx_ps[32 * j:32 * j + VW, s * S:(s + 1) * S], v_sb[0:n, c % 2, t, h, :],
                                     ex[0:n, u % NE, q // HG, j * S:(j + 1) * S],
                                     start=u == 0 and s == 0, stop=u >= UPB - 2 and s == 2 * half + 1,
                                     skip_group_check=True)
                last.then_inc(pv_done, 1)

            def attend(b, first_batch, last_batch):
                for u in range(UPB):
                    c, v = divmod(u, UPC)
                    g = b * CPB + c
                    more = not (last_batch and c == CPB - 1)
                    scores(b, u, g)
                    if v < 2 and more:
                        project_keys(g + 1, c + 1, v)
                    if v in (2, 5) and more:
                        project_values(g + 1, c + 1, 0 if v == 2 else 2)
                    if u % 2 == 1:
                        for w in (u - LAG, u - LAG + 1):
                            if w >= 0:
                                weigh_values(b, w)
                            elif not first_batch:
                                weigh_values(b - 1, w + UPB)
                    if v == 3 and more:
                        project_values(g + 1, c + 1, 1)
            project_keys(0, 0, 0)
            project_keys(0, 0, 1)
            for t in range(NKT):
                project_values(0, 0, t)
            attend(0, True, False)
            with pe.Fori(1, B - 1) as b:
                attend(b, False, False)
            attend(B - 1, False, True)
            for u in range(UPB - LAG + 1, UPB):
                weigh_values(B - 1, u)

            pe.wait_ge(ctx_saved, B)
            pe.wait_ge(params_loaded, 16 * 20)

            def spread(i, j):
                src = qc[:, :, i * P:(i + 1) * P] if isinstance(i, int) else qc[:, :, bass.ds(i * P, P)]
                pe.matmul(ps[:, j % 2].rearrange("p (g s) -> p g s", g=G), row_of_sum[:], src,
                          start=True, stop=True).then_inc(sums_spread, 1)
            def output_block(k):
                for j in range(BT):
                    i = k * BT + j
                    if j == 0:
                        used(pe, ctx_normed, i)
                        spread(i, 0)
                    if j < BT - 1:
                        used(pe, ctx_normed, i)
                        spread(i + 1, j + 1)
                    pe.wait_ge(ctx_normed, i + 1)
                    used(pe, delta_ready, i if j == 0 else i - 1)
                    for s in range(G):
                        last = pe.matmul(ps[:, 2 + j % 2, 0:D], ctxn[:, j % 2, s], wo_sb[:, s], start=s == 0,
                                         stop=s == G - 1)
                    last.then_inc(o_projected, 1)
            output_block(0)
            with pe.Fori(1, NBLK) as k:
                output_block(k)

            pe.wait_ge(delta_ready, NT)

            def logits(i):
                pe.wait_ge(xts_ready, i + 1)
                if i >= 2:
                    pe.wait_ge(logits_kept, i - 1)
                for kc in range(KC):
                    last = pe.matmul(ps[:, 2 + i % 2, 0:E], xts[:, i % 2, kc], rw_sb[:, kc], start=kc == 0,
                                     stop=kc == KC - 1)
                last.then_inc(logits_done, 1)
            for i in range(NT):
                pe.wait_ge(xn_ready, i + 1)
                if i >= 2:
                    pe.wait_ge(xt_kept, i - 1)
                for kc in range(KC):
                    last = pe.transpose(ps[:, i % 2, kc * P:(kc + 1) * P], xn[:, i % 2, kc * P:(kc + 1) * P], ident[:])
                last.then_inc(xn_transposed, 1)
                if i >= 1:
                    logits(i - 1)
            logits(NT - 1)

            pe.wait_ge(xt_kept, NT)
            pe.wait_ge(logits_kept, NT)
            pe.wait_ge(stage_split, 2 * len(pieces))

            def gate_up(i, slot, e):
                if not (isinstance(i, int) and i == 0 and e < 2):
                    pe.wait_ge(act_ready, i * E + e - 1)
                parts(ps[:, e % 2, 0:2 * I], lambda p, kc: xs_p[:, slot, p, kc, :],
                      lambda p, kc: gu_p[:, p, kc, e, :], KC).then_inc(gu_done, 1)

            def transpose_hidden(i, slot, q):
                if q == 0:
                    pe.wait_ge(act_ready, i * E + E)
                if not (isinstance(i, int) and i == 0):
                    pe.wait_ge(actt_lo, i * 3 - 3 + q + 1)
                n = min(4, NF - 4 * q)
                for f in range(4 * q, 4 * q + n):
                    last = pe.transpose(ps[:, 2 + q, (f % 4) * P:(f % 4 + 1) * P], act[:, slot, f * P:(f + 1) * P],
                                        ident[:])
                last.then_inc(act_transposed, 1)

            def down_proj(i):
                pe.wait_ge(actt_lo, i * 3 + 3)
                if not (isinstance(i, int) and i == 0):
                    pe.wait_ge(y_ready, i)
                parts(ps[:, 5, 0:D], lambda p, f: actt_p[:, p, f, :], lambda p, f: dn_p[:, p, f, :],
                      NF).then_inc(down_done, 1)

            def expert_tile(i, slot, has_before):
                pe.wait_ge(xs_lo, i + 1)
                for e in range(E):
                    gate_up(i, slot, e)
                    if has_before and 1 <= e < 4:
                        transpose_hidden(i - 1, 1 - slot, e - 1)
                    if has_before and e == 6:
                        down_proj(i - 1)
            expert_tile(0, 0, False)
            expert_tile(1, 1, True)
            with pe.Fori(1, NT // 2) as r:
                expert_tile(r * 2, 0, True)
                expert_tile(r * 2 + 1, 1, True)
            expert_tile(NT - 1, 0, True)
            for q in range(3):
                transpose_hidden(NT - 1, 0, q)
            down_proj(NT - 1)


def kernel(x, ctx_2048, mask_BxS2_ik0, g_xattn, g_ffn, L0_xattn_Wq, L0_xattn_bq, L0_xattn_Wk, L0_xattn_bk,
           L0_xattn_Wv, L0_xattn_bv, L0_xattn_Wo, L0_xattn_bo, L0_xattn_ln_gamma, L0_xattn_ln_beta,
           L0_xattn_residual_scale, L0_ffn_router_w, L0_ffn_gate_w, L0_ffn_up_w, L0_ffn_down_w):
    import concourse.bacc as bacc
    from concourse.bass_utils import run_bass_kernel_spmd

    def lay(a):
        return np.ascontiguousarray(a)

    def weight(w):
        w = np.asarray(w)
        return lay(w.T.reshape(KC, P, w.shape[0]).transpose(1, 0, 2))

    def experts_in(w):
        return lay(np.asarray(w).transpose(2, 0, 1).reshape(KC, P, E, I).transpose(1, 0, 2, 3))

    wo = np.asarray(L0_xattn_Wo).T.reshape(G, HG, HD, D)
    bq = np.asarray(L0_xattn_bq).reshape(G, GR)
    data = {
        "x": lay(np.asarray(x).reshape(TOK, D)),
        "ctx_t": lay(np.asarray(ctx_2048).reshape(NCH, CHUNK, KC, P).transpose(0, 3, 2, 1)),
        "mask_t": lay(np.asarray(mask_BxS2_ik0).reshape(NCH, CHUNK).T),
        "g_xattn": lay(np.asarray(g_xattn).reshape(1)),
        "g_ffn": lay(np.asarray(g_ffn).reshape(1)),
        "wq": weight(L0_xattn_Wq),
        "bq": lay(np.concatenate([bq, bq], axis=1).T),
        "wk": weight(L0_xattn_Wk),
        "bk": lay(np.asarray(L0_xattn_bk).reshape(KC, P).T),
        "wv": weight(L0_xattn_Wv),
        "bv": lay(L0_xattn_bv),
        "wo": lay(wo.transpose(1, 2, 0, 3)),
        "bo": lay(L0_xattn_bo),
        "gamma": lay(L0_xattn_ln_gamma),
        "beta": lay(L0_xattn_ln_beta),
        "rs": lay(np.asarray(L0_xattn_residual_scale).reshape(1)),
        "router": weight(L0_ffn_router_w),
        "gate": experts_in(L0_ffn_gate_w),
        "up": experts_in(L0_ffn_up_w),
        "down": lay(np.asarray(L0_ffn_down_w).transpose(0, 2, 1).reshape(NF, P, D).transpose(1, 0, 2)),
    }
    nc = bacc.Bacc("TRN2", target_bir_lowering=False, num_devices=1)
    args = [nc.dram_tensor(name, a.shape, mybir.dt.from_np(a.dtype), kind="ExternalInput").ap()
            for name, a in data.items()]
    out = nc.dram_tensor("out", (TOK, D), F32, kind="ExternalOutput").ap()
    build(nc, *args, out)
    r = run_bass_kernel_spmd(nc, [data], core_ids=[0])
    return r.results[0]["out"].reshape(B, S, D)
```

```python
from contextlib import ExitStack

import numpy as np

import concourse.bass as bass
from concourse import mybir

F32 = mybir.dt.float32
F32R = mybir.dt.float32r
I32 = mybir.dt.int32
ALU = mybir.AluOpType
ACT = mybir.ActivationFunctionType
AX_X = mybir.AxisListType.X

P = 128
B, S, T, D = 32, 100, 1444, 256
H, HD = 16, 16
E, I = 8, 176
EPS_LN = 1e-5
EPS_PROBS = 1e-8
SCORE_CLIP = 50.0
RES_SCALE_MAX = 0.3
EXP_HI = float(np.exp(np.float64(SCORE_CLIP)))
EXP_LO = float(np.exp(np.float64(-SCORE_CLIP)))

KC = D // P
TOK = B * S
NT = TOK // P
BT = 5
NBLK = NT // BT

CPB = 4
CHUNK = T // CPB
CW = CHUNK + 1
KEYS = [121, 120, 120]
KOFF = [0, 121, 241]
NKT = len(KEYS)
G, HG = 4, 4
GR = HG * HD
UPC = 2 * NKT
UPB = UPC * CPB
NCH = B * CPB
NE = 4
LAG = 3
VW = HD + 1

NPARAM = 11 + 3 + NKT
NF = E * I // P
PIECE = 4 * I
NGU = KC * E * 2 * I // PIECE
NDN = NF * D // PIECE
NPIECE = NGU + NDN
LOADS = 4
DEPTH = 9
DELTA_ROOT, X1_ROOT = 4, 6
FIRST_PIECE = 3


def build(nc, x, ctx_t, mask_t, g_xattn, g_ffn, wq, bq, wk, bk, wv, bv, wo, bo, gamma, beta, rs, router,
          w_ffn, out):
    top = ExitStack()

    def sem(name):
        return top.enter_context(nc.semaphore(name))

    def sb(stack, name, shape, dt=F32):
        return stack.enter_context(nc.sbuf_tensor(name, shape, dt))

    with top:
        ps = top.enter_context(nc.psum_tensor("ps", [P, 8, 512], F32))
        psf = ps[:].rearrange("p b n -> p (b n)")
        x_all = sb(top, "x_all", [P, NT, D])
        qc = sb(top, "qc", [P, G, TOK])
        ident = sb(top, "ident", [P, P])
        wo_sb = sb(top, "wo_sb", [P, KC, D])
        gam = sb(top, "gam", [P, D])
        bet = sb(top, "bet", [P, D])
        bo_sb = sb(top, "bo_sb", [P, D])
        bv_sb = sb(top, "bv_sb", [P, D])
        bq_sb = sb(top, "bq_sb", [P, G])
        bk_sb = sb(top, "bk_sb", [P, KC])
        rw_sb = sb(top, "rw_sb", [P, KC, E])
        scal = sb(top, "scal", [P, 3])
        tg = sb(top, "tg", [P, 2])
        rsc = sb(top, "rsc", [P, 1])
        stats = sb(top, "stats", [P, NT, 6])
        mean = sb(top, "mean", [P, NT])
        var = sb(top, "var", [P, NT])
        tmp_s = sb(top, "tmp_s", [P, 2, NT])
        rstd = sb(top, "rstd", [P, NT])
        eps_ln = sb(top, "eps_ln", [P, 1])
        minus_half = sb(top, "minus_half", [P, 1])
        lg = sb(top, "lg", [P, NT, E])

        params_loaded = sem("params_loaded")
        x_loaded = [sem(f"x_loaded{k}") for k in range(NBLK)]
        consts_made = sem("consts_made")
        chain = sem("chain")
        std_ready = sem("std_ready")
        gates_ready = sem("gates_ready")
        gates_applied = sem("gates_applied")
        rsc_ready = sem("rsc_ready")
        var_ready = sem("var_ready")

        attn = ExitStack()
        mask_i = sb(attn, "mask_i", [P, NKT, NCH], I32)
        m_scale = sb(attn, "m_scale", [P, NKT, NCH])
        m_bias = sb(attn, "m_bias", [P, NKT, NCH])
        w_raw = sb(attn, "w_raw", [P, KC, D])
        w_raw2 = sb(attn, "w_raw2", [P, KC, D])
        w_raw3 = sb(attn, "w_raw3", [P, KC, D])
        wk_p = sb(attn, "wk_p", [P, 2, KC, D], F32R)
        wv_p = sb(attn, "wv_p", [P, 2, KC, D], F32R)
        head_mask = sb(attn, "head_mask", [P, HG, S])
        zeros = sb(attn, "zeros", [P, 512])

        first = ExitStack()
        wq_p = sb(first, "wq_p", [P, 2, KC, G, 2, GR], F32R)
        hs = sb(first, "hs", [P, BT, D])
        hst_p = sb(first, "hst_p", [P, 2, KC, BT * P], F32R)
        first.close()

        at_raw = sb(attn, "at_raw", [P, 2, KC, CHUNK])
        at_p = sb(attn, "at_p", [P, 2, 2, KC, CW], F32R)
        kt_p = sb(attn, "kt_p", [P, 2, G, CW], F32R)
        v_sb = sb(attn, "v_sb", [P, 2, NKT, H, VW])
        ex = sb(attn, "ex", [P, NE, 2, HG * S])
        qbd = sb(attn, "qbd", [P, 2, 2, G, HG, S], F32R)
        qprod = sb(attn, "qprod", [P, 2, HG, S])
        attn.close()

        ffn = ExitStack()
        xn = sb(ffn, "xn", [P, 2, D])
        xts = sb(ffn, "xts", [P, 2, KC, P])
        w_p = sb(ffn, "w_p", [P, 2, NPIECE, PIECE], F32R)
        outp = ExitStack()
        w_in = sb(outp, "w_in", [P, NPIECE, PIECE])
        stg = sb(outp, "stg", [P, 2, G, P])
        ctxn = sb(outp, "ctxn", [P, 2, D])
        ctxt = sb(outp, "ctxt", [P, 2, KC, P])
        dlt = sb(outp, "dlt", [P, 2, D])
        zed = sb(outp, "zed", [P, 2, D])
        den = sb(outp, "den", [P, 3, 2, H])
        st_d = sb(outp, "st_d", [P, 2, 6])
        st_x = sb(outp, "st_x", [P, 2, 6])
        mv = sb(outp, "mv", [P, 2, 2, 2])
        var_eps = sb(outp, "var_eps", [P, 2, 2])
        rstds = sb(outp, "rstds", [P, 2, 2])
        outp.close()
        actt_p = sb(ffn, "actt_p", [P, 2, NF, P], F32R)
        act = sb(ffn, "act", [P, 2, NF * P])
        xs_p = sb(ffn, "xs_p", [P, 2, 2, KC, P], F32R)
        sil = sb(ffn, "sil", [P, 3, I])
        y_out = sb(ffn, "y_out", [P, 2, D])
        r_a = sb(ffn, "r_a", [P, NT, E])
        r_b = sb(ffn, "r_b", [P, NT, E])
        iota_e = sb(ffn, "iota_e", [P, NT, E])
        r_m = sb(ffn, "r_m", [P, 4, NT])
        ffn.close()

        hs_ready = sem("hs_ready")
        hs_transposed = sem("hs_transposed")
        hst_hi = sem("hst_hi")
        hst_lo = sem("hst_lo")
        wq_split = sem("wq_split")
        q_projected = sem("q_projected")
        q_stored = sem("q_stored")
        w_split = sem("w_split")
        mask_ready = sem("mask_ready")
        pads_set = sem("pads_set")
        at_loaded = [sem("at_loaded0"), sem("at_loaded1")]
        at_split = sem("at_split")
        k_projected = sem("k_projected")
        k_hi = sem("k_hi")
        k_lo = sem("k_lo")
        v_projected = sem("v_projected")
        v_ready = sem("v_ready")
        q_built = sem("q_built")
        pool_chain = sem("pool_chain")
        scored = sem("scored")
        exped = sem("exped")
        clipped = sem("clipped")
        pv_done = sem("pv_done")
        ctx_cleared = sem("ctx_cleared")
        ctx_saved = sem("ctx_saved")
        staged = sem("staged")
        stage_transposed = sem("stage_transposed")
        eps_sums = sem("eps_sums")
        den_ready = sem("den_ready")
        recip_ready = sem("recip_ready")
        ctx_normed = sem("ctx_normed")
        ctxn_transposed = sem("ctxn_transposed")
        ctxt_ready = sem("ctxt_ready")
        o_projected = sem("o_projected")
        delta_ready = sem("delta_ready")
        delta_stats = sem("delta_stats")
        delta_var = sem("delta_var")
        zed_ready = sem("zed_ready")
        x1_ready = sem("x1_ready")
        x1_stats = sem("x1_stats")
        x1_var = sem("x1_var")
        vars_widened = sem("vars_widened")
        roots_ready = sem("roots_ready")
        xn_ready = sem("xn_ready")
        xn_transposed = sem("xn_transposed")
        xts_ready = sem("xts_ready")
        xt_kept = sem("xt_kept")
        logits_done = sem("logits_done")
        logits_kept = sem("logits_kept")
        beta_added = sem("beta_added")
        w_loaded = [sem(f"w_loaded{k}") for k in range(LOADS)]
        w_hi = sem("w_hi")
        w_lo = sem("w_lo")
        gap_ready = sem("gap_ready")
        gap_exped = sem("gap_exped")
        combine_ready = sem("combine_ready")
        xs_hi = sem("xs_hi")
        xs_lo = sem("xs_lo")
        gu_done = sem("gu_done")
        silu_done = sem("silu_done")
        act_ready = sem("act_ready")
        act_transposed = sem("act_transposed")
        actt_hi = sem("actt_hi")
        actt_lo = sem("actt_lo")
        down_done = sem("down_done")
        y_ready = sem("y_ready")
        y_stored = [sem("y_stored0"), sem("y_stored1")]

        def tps(kc, lo, n):
            return psf[:, kc * 1024 + lo:kc * 1024 + lo + n]

        def qps(g, half):
            return ps[:, 4 + 2 * (g % 2) + half, 0:BT * P // 2]

        def kps(m):
            return ps[:, m, 0:CW]
        vps = ps[:, 2, 0:D]
        ctx_ps = ps[:, 3, 0:G * S]

        def sps(u):
            return ps[:, 4 + 2 * (u % 2):6 + 2 * (u % 2), 0:HG * S]

        def gu_ps(e):
            return ps[:, (0, 1, 6, 7)[e % 4]]

        def used(eng, semaphore, value):
            if not isinstance(value, int) or value > 0:
                eng.wait_ge(semaphore, value)

        block = top.enter_context(nc.Block())

        def gu_w(p, kc, e):
            return w_p[:, p, 0:NGU].rearrange("p n w -> p (n w)")[:, (kc * E + e) * 2 * I:(kc * E + e + 1) * 2 * I]

        def dn_w(p, f):
            return w_p[:, p, NGU:NPIECE].rearrange("p n w -> p (n w)")[:, f * D:(f + 1) * D]

        def tile_steps(eng, step):
            start = DEPTH + 2
            stop = start + (NT - start) // 2 * 2
            for t in range(start):
                step(t, t % 2)
            with eng.Fori(0, (stop - start) // 2) as r:
                step(r * 2 + start, start % 2)
                step(r * 2 + start + 1, (start + 1) % 2)
            for t in range(stop, NT + DEPTH):
                step(t, t % 2)

        def exists(i):
            return not isinstance(i, int) or 0 <= i < NT

        def tile_cols(ap, i):
            return ap[:, :, i * P:(i + 1) * P] if isinstance(i, int) else ap[:, :, bass.ds(i * P, P)]

        def one(ap, i):
            return ap[:, i] if isinstance(i, int) else ap[:, bass.ds(i, 1)].rearrange("p o n -> p (o n)")

        def piece(part, k):
            return one(w_p[:, part], k)

        def piece_of_step(t, slot):
            if slot != FIRST_PIECE % 2:
                return None
            if not isinstance(t, int):
                return ((t - FIRST_PIECE) // 2)
            k = (t - FIRST_PIECE) // 2
            return k if 0 <= k < NPIECE else None

        @block.sync
        def _(sp):
            for k in range(NBLK):
                sp.dma_start(x_all[:, k * BT:(k + 1) * BT, :],
                             x.rearrange("(n p) d -> p n d", p=P)[:, k * BT:(k + 1) * BT, :]).then_inc(x_loaded[k], 16)
            plain = [(w_raw, wq), (w_raw2, wk), (w_raw3, wv), (wo_sb, wo), (bq_sb, bq), (bk_sb, bk), (rw_sb, router)]
            for dst, src in plain:
                sp.dma_start(dst[:], src).then_inc(params_loaded, 16)
            for dst, src in ((bv_sb, bv), (bo_sb, bo), (gam, gamma), (bet, beta)):
                sp.dma_start(dst[:], src.partition_broadcast(P)).then_inc(params_loaded, 16)
            for k, src in enumerate((g_xattn, g_ffn, rs)):
                sp.dma_start(scal[:, k:k + 1], src.partition_broadcast(P)).then_inc(params_loaded, 16)
            for t in range(NKT):
                sp.dma_start(mask_i[0:KEYS[t], t, :], mask_t[KOFF[t]:KOFF[t] + KEYS[t], :]).then_inc(params_loaded, 16)

            def load_chunk(b, c):
                sp.dma_start(at_raw[:, c % 2], ctx_t[b * CPB + c] if isinstance(b, int)
                             else ctx_t[bass.ds(b * CPB + c, 1)].rearrange("o p k n -> (o p) k n")
                             ).then_inc(at_loaded[c % 2], 16)
            sp.wait_ge(q_stored, G * NBLK)
            for c in range(CPB):
                if c >= 2:
                    sp.wait_ge(at_split, 2 * (c - 1))
                load_chunk(0, c)
            with sp.Fori(1, B) as b:
                for c in range(CPB):
                    sp.wait_ge(at_split, b * 2 * CPB + 2 * (c - 1))
                    load_chunk(b, c)
            sp.wait_ge(ctx_saved, B)
            for k in range(LOADS):
                n = NPIECE // LOADS
                sp.dma_start(w_in[:, k * n:(k + 1) * n], w_ffn[:, k * n:(k + 1) * n]).then_inc(w_loaded[k], 16)

            def store(i, slot):
                sp.wait_ge(y_ready, i + 1)
                dst = out[i * P:(i + 1) * P, :] if isinstance(i, int) else out[bass.ds(i * P, P), :]
                sp.dma_start(dst, y_out[:, slot, :]).then_inc(y_stored[slot], 16)
            with sp.Fori(0, NT // 2) as r:
                store(r * 2, 0)
                store(r * 2 + 1, 1)
            store(NT - 1, 0)
            sp.wait_ge(y_stored[0], 16 * (NT // 2 + 1))
            sp.wait_ge(y_stored[1], 16 * (NT // 2))

        @block.gpsimd
        def _(pool):
            nc.gpsimd.memset(ident[:], 1.0).then_inc(pool_chain, 1)
            nc.gpsimd.memset(head_mask[:], 1.0).then_inc(pool_chain, 1)
            pool.wait_ge(pool_chain, 2)
            nc.gpsimd.affine_select(out=ident[:], in_=ident[:], compare_op=ALU.is_equal, fill=0.0, base=0,
                                    pattern=[[-1, P]], channel_multiplier=1).then_inc(consts_made, 1)
            for half in range(2):
                w = head_mask[half * GR:(half + 1) * GR]
                nc.gpsimd.affine_select(out=w, in_=w, compare_op=ALU.is_ge, fill=0.0, base=0,
                                        pattern=[[-HD, HG], [0, S]], channel_multiplier=1).then_inc(pool_chain, 1)
                pool.wait_ge(pool_chain, 3 + 2 * half)
                nc.gpsimd.affine_select(out=w, in_=w, compare_op=ALU.is_ge, fill=0.0, base=HD - 1,
                                        pattern=[[HD, HG], [0, S]], channel_multiplier=-1).then_inc(pool_chain, 1)
            pool.wait_ge(pool_chain, 6)
            BASE = 6

            def build_q(b, slot):
                for g in range(G):
                    k = b * (2 * G) + BASE + 2 * g
                    q = qc[:, g, b * S:(b + 1) * S] if isinstance(b, int) else qc[:, g, bass.ds(b * S, S)]
                    hi = qbd[:, slot, 0, g] if isinstance(b, int) else \
                        qbd[:, bass.ds(slot, 1), 0, g].rearrange("p o h s -> p (o h) s")
                    lo = qbd[:, slot, 1, g] if isinstance(b, int) else \
                        qbd[:, bass.ds(slot, 1), 1, g].rearrange("p o h s -> p (o h) s")
                    prod = qprod[:, g % 2]
                    nc.gpsimd.tensor_tensor(prod, q.unsqueeze(1).to_broadcast([P, HG, S]), head_mask[:],
                                            ALU.mult).then_inc(pool_chain, 1)
                    pool.wait_ge(pool_chain, k + 1)
                    nc.gpsimd.tensor_copy(hi, prod).then_inc(pool_chain, 1)
                    pool.wait_ge(pool_chain, k + 2)
                    nc.gpsimd.tensor_tensor(lo, prod, hi.bitcast(F32), ALU.subtract).then_inc(q_built, 1)

            pool.wait_ge(q_stored, G * NBLK)
            build_q(0, 0)
            build_q(1, 1)
            pool.wait_ge(gates_applied, 2)
            with pool.Fori(0, NT) as i:
                nc.gpsimd.tensor_tensor(one(x_all, i), one(x_all, i), bet[:], ALU.add).then_inc(beta_added, 1)
            with pool.Fori(2, B) as b:
                pool.wait_ge(scored, b * UPB - UPB)
                build_q(b, b % 2)

            def roots(t, slot):
                lo = 0 if exists(t - DELTA_ROOT) else 1
                hi = 2 if exists(t - X1_ROOT) else 1
                if lo >= hi:
                    return
                if lo == 0:
                    pool.wait_ge(delta_var, t - DELTA_ROOT + 1)
                    used(pool, x1_ready, t - DELTA_ROOT - 1)
                if hi == 2:
                    pool.wait_ge(x1_var, t - X1_ROOT + 1)
                    used(pool, xn_ready, t - X1_ROOT - 1)
                nc.gpsimd.tensor_tensor(var_eps[:, slot, lo:hi], mv[:, slot, lo:hi, 1],
                                        eps_ln[:].to_broadcast([P, hi - lo]), ALU.add).then_inc(vars_widened, 1)
                pool.wait_ge(vars_widened, t - DELTA_ROOT + 1)
                nc.gpsimd.tensor_tensor(rstds[:, slot, lo:hi], var_eps[:, slot, lo:hi],
                                        minus_half[:].to_broadcast([P, hi - lo]), ALU.pow).then_inc(roots_ready, 1)

            def split_low(k):
                pool.wait_ge(w_hi, k + 1)
                nc.gpsimd.tensor_tensor(piece(1, k), one(w_in, k), piece(0, k).bitcast(F32),
                                        ALU.subtract).then_inc(w_lo, 1)

            def step(t, slot):
                roots(t, slot)
                k = piece_of_step(t, slot)
                if k is not None:
                    split_low(k)
            pool.wait_ge(ctx_saved, B)
            tile_steps(pool, step)

        @block.vector
        def _(dve):
            n_chain = [0]

            def linked(ins):
                n_chain[0] += 1
                ins.then_inc(chain, 1)
                dve.wait_ge(chain, n_chain[0])

            def mean_and_var():
                linked(dve.tensor_tensor(mean[:], stats[:, :, 1], stats[:, :, 4], ALU.add))
                linked(dve.tensor_scalar(mean[:], mean[:], 0.5, None, ALU.mult))
                linked(dve.tensor_tensor(tmp_s[:, 0], stats[:, :, 1], stats[:, :, 4], ALU.subtract))
                linked(dve.scalar_tensor_tensor(out=tmp_s[:, 1], in0=tmp_s[:, 0], scalar=0.25, in1=tmp_s[:, 0],
                                                op0=ALU.mult, op1=ALU.mult))
                linked(dve.tensor_tensor(tmp_s[:, 0], stats[:, :, 2], stats[:, :, 5], ALU.add))
                dve.scalar_tensor_tensor(out=var[:], in0=tmp_s[:, 0], scalar=1.0 / D, in1=tmp_s[:, 1],
                                         op0=ALU.mult, op1=ALU.add).then_inc(var_ready, 1)

            dve.memset(minus_half[:], -0.5).then_inc(pads_set, 1)
            dve.memset(eps_ln[:], EPS_LN).then_inc(var_ready, 1)
            dve.memset(zeros[:], 0.0).then_inc(pads_set, 1)
            for k in range(NBLK):
                dve.wait_ge(x_loaded[k], 16)
                for j in range(BT):
                    n = k * BT + j
                    last = dve.bn_stats(stats[:, n, :], x_all[:, n, :])
            linked(last)
            mean_and_var()
            dve.wait_ge(params_loaded, 16 * NPARAM)
            raw_g = w_raw[:].rearrange("p k (g c) -> p k g c", g=G)
            for twin in range(2):
                dve.tensor_copy(wq_p[:, 0, :, :, twin, :], raw_g).then_inc(wq_split, 1)
            dve.wait_ge(wq_split, 2)
            for twin in range(2):
                for kc in range(KC):
                    dve.tensor_tensor(wq_p[:, 1, kc, :, twin, :], raw_g[:, kc], wq_p[:, 0, kc, :, twin, :].bitcast(F32),
                                      ALU.subtract).then_inc(wq_split, 1)
            dve.tensor_copy(wk_p[:, 0], w_raw2[:]).then_inc(w_split, 1)
            dve.tensor_copy(wv_p[:, 0], w_raw3[:]).then_inc(w_split, 1)
            dve.wait_ge(w_split, 2)
            dve.tensor_tensor(wk_p[:, 1], w_raw2[:], wk_p[:, 0].bitcast(F32), ALU.subtract).then_inc(w_split, 1)
            dve.tensor_tensor(wv_p[:, 1], w_raw3[:], wv_p[:, 0].bitcast(F32), ALU.subtract).then_inc(w_split, 1)
            inv = 1.0 / float(np.sqrt(HD))
            for t in range(NKT):
                linked(dve.tensor_scalar(m_scale[0:KEYS[t], t], mask_i[0:KEYS[t], t], 0.5, inv, ALU.is_gt, ALU.mult))
                dve.tensor_scalar(m_bias[0:KEYS[t], t], m_scale[0:KEYS[t], t], SCORE_CLIP / inv, -SCORE_CLIP,
                                  ALU.mult, ALU.add).then_inc(mask_ready, 1)
            dve.wait_ge(gates_ready, 2)
            dve.tensor_scalar(rsc[:], scal[:, 2:3], 0.0, RES_SCALE_MAX, ALU.max, ALU.min).then_inc(rsc_ready, 1)
            for v in (gam, bet):
                dve.tensor_scalar(v[:], v[:], tg[:, 0:1], None, ALU.mult).then_inc(gates_applied, 1)
            dve.wait_ge(std_ready, 1)
            linked(dve.reciprocal(rstd[:], rstd[:]))
            for k in range(NBLK):
                for j in range(BT):
                    n = k * BT + j
                    if k >= 1:
                        dve.wait_ge(hs_transposed, k)
                    dve.tensor_scalar(hs[:, j, :], x_all[:, n, :], mean[:, n:n + 1], rstd[:, n:n + 1],
                                      ALU.subtract, ALU.mult).then_inc(hs_ready, 1)
                for kc in range(KC):
                    dve.wait_ge(hst_hi, KC * k + kc + 1)
                    dve.tensor_tensor(hst_p[:, 1, kc], tps(kc, 0, BT * P), hst_p[:, 0, kc].bitcast(F32),
                                      ALU.subtract).then_inc(hst_lo, 1)

            dve.wait_ge(q_stored, G * NBLK)
            dve.memset(v_sb[:, :, :, :, HD:VW], 1.0).then_inc(pads_set, 1)
            dve.memset(at_p[:, :, :, :, CHUNK:CW].bitcast(F32), 0.0).then_inc(pads_set, 1)

            def split_hi(g, c):
                s = c % 2
                dve.wait_ge(at_loaded[s], (g - s) * 8 + 16)
                if not (isinstance(g, int) and g < 2):
                    dve.wait_ge(v_projected, NKT * (g - 1))
                dve.tensor_copy(at_p[:, s, 0, :, 0:CHUNK], at_raw[:, s]).then_inc(at_split, 1)

            def split_lo(g, c):
                s = c % 2
                dve.wait_ge(at_split, g * 2 + 1)
                dve.tensor_tensor(at_p[:, s, 1, :, 0:CHUNK], at_raw[:, s], at_p[:, s, 0, :, 0:CHUNK].bitcast(F32),
                                  ALU.subtract).then_inc(at_split, 1)

            def key_lo(g, c, m):
                for h in range(2):
                    grp = 2 * m + h
                    dve.wait_ge(k_hi, g * G + grp + 1)
                    dve.scalar_tensor_tensor(out=kt_p[GR:P, c % 2, grp, :], in0=kps(m)[h * GR:(h + 1) * GR],
                                             scalar=bk_sb[h * GR:(h + 1) * GR, m:m + 1],
                                             in1=kt_p[0:GR, c % 2, grp, :].bitcast(F32),
                                             op0=ALU.add, op1=ALU.subtract).then_inc(k_lo, 1)

            def value_tile(g, c, t):
                dve.wait_ge(v_projected, g * NKT + t + 1)
                if not (isinstance(g, int) and g < 2):
                    dve.wait_ge(pv_done, (g - 2) * UPC + 2 * t + 2)
                n = KEYS[t]
                dve.tensor_tensor(v_sb[0:n, c % 2, t, :, 0:HD], vps[0:n].rearrange("p (h d) -> p h d", h=H),
                                  bv_sb[0:n].rearrange("p (h d) -> p h d", h=H), ALU.add).then_inc(v_ready, 1)

            def clip(U, u):
                dve.wait_ge(exped, U + 1)
                n = KEYS[(u % UPC) // 2]
                e = ex[0:n, u % NE]
                dve.tensor_scalar(e, e, EXP_LO, EXP_HI, ALU.max, ALU.min).then_inc(clipped, 1)

            def attend(b, last_batch):
                for u in range(UPB):
                    c, v = divmod(u, UPC)
                    g = b * CPB + c
                    more = not (last_batch and c == CPB - 1)
                    if v in (2, 5) and more:
                        value_tile(g + 1, c + 1, 0 if v == 2 else 2)
                    clip(b * UPB + u, u)
                    if v == 3 and more:
                        value_tile(g + 1, c + 1, 1)
                    if v < 2 and more:
                        key_lo(g + 1, c + 1, v)
                    if not (last_batch and c >= CPB - 2):
                        if v == 2:
                            split_hi(g + 2, c)
                        if v == 4:
                            split_lo(g + 2, c)
            for g in range(2):
                split_hi(g, g)
                split_lo(g, g)
            key_lo(0, 0, 0)
            key_lo(0, 0, 1)
            for t in range(NKT):
                value_tile(0, 0, t)
            attend(0, False)
            with dve.Fori(1, B - 1) as b:
                attend(b, False)
            attend(B - 1, True)

            def eps_times_sum(i, slot):
                dve.wait_ge(stage_transposed, i + 1)
                dve.tensor_scalar(den[:, 0, slot], sums(slot), EPS_PROBS, None, ALU.mult).then_inc(eps_sums, 1)

            def sums(slot):
                return ps[:, slot].rearrange("p (h c) -> p h c", c=32)[:, :, HD]

            def denominator(i, slot):
                dve.wait_ge(eps_sums, i + 1)
                dve.tensor_tensor(den[:, 1, slot], sums(slot), den[:, 0, slot], ALU.add).then_inc(den_ready, 1)

            def factor(i, slot):
                dve.wait_ge(den_ready, i + 1)
                dve.reciprocal(den[:, 2, slot], den[:, 1, slot]).then_inc(recip_ready, 1)

            def norm_ctx(i, slot):
                dve.wait_ge(recip_ready, i + 1)
                used(dve, ctxn_transposed, i - 1)
                dve.tensor_tensor(ctxn[:, slot].rearrange("p (h d) -> p h d", h=H),
                                  ps[:, slot].rearrange("p (h c) -> p h c", c=32)[:, :, 0:HD],
                                  den[:, 2, slot].unsqueeze(2).to_broadcast([P, H, HD]), ALU.mult
                                  ).then_inc(ctx_normed, 1)

            def stats_of_delta(i, slot):
                dve.wait_ge(delta_ready, i + 1)
                dve.bn_stats(st_d[:, slot], dlt[:, slot]).then_inc(delta_stats, 1)

            def var_of_delta(i, slot):
                dve.wait_ge(delta_stats, i + 1)
                used(dve, roots_ready, i - 1)
                used(dve, zed_ready, i - 1)
                dve.nop(nofuse=True)
                dve.bn_aggr(mv[:, slot, 0], st_d[:, slot]).then_inc(delta_var, 1)

            def centre_delta(i, slot):
                dve.wait_ge(delta_var, i + 1)
                dve.scalar_tensor_tensor(out=zed[:, slot], in0=dlt[:, slot], scalar=mv[:, slot, 0, 0:1], in1=gam[:],
                                         op0=ALU.subtract, op1=ALU.mult).then_inc(zed_ready, 1)

            def first_residual(i, slot):
                dve.wait_ge(zed_ready, i + 1)
                dve.wait_ge(roots_ready, i + 1)
                dve.wait_ge(beta_added, NT)
                dve.scalar_tensor_tensor(out=one(x_all, i), in0=zed[:, slot], scalar=rstds[:, slot, 0:1],
                                         in1=one(x_all, i), op0=ALU.mult, op1=ALU.add).then_inc(x1_ready, 1)

            def stats_of_x1(i, slot):
                dve.wait_ge(x1_ready, i + 1)
                dve.nop(nofuse=True)
                dve.bn_stats(st_x[:, slot], one(x_all, i)).then_inc(x1_stats, 1)

            def var_of_x1(i, slot):
                dve.wait_ge(x1_stats, i + 1)
                used(dve, roots_ready, i + X1_ROOT - DELTA_ROOT - 1)
                used(dve, xn_ready, i - 1)
                dve.nop(nofuse=True)
                dve.bn_aggr(mv[:, slot, 1], st_x[:, slot]).then_inc(x1_var, 1)

            def norm_x1(i, slot):
                dve.wait_ge(roots_ready, i + X1_ROOT - DELTA_ROOT + 1)
                used(dve, xn_transposed, i - 1)
                dve.tensor_scalar(xn[:, slot], one(x_all, i), mv[:, slot, 1, 0:1], rstds[:, slot, 1:2],
                                  ALU.subtract, ALU.mult).then_inc(xn_ready, 1)

            def keep_logits(i, slot):
                dve.wait_ge(logits_done, i + 1)
                dve.tensor_copy(one(lg, i), ps[:, 6 + slot, D:D + E]).then_inc(logits_kept, 1)

            def step(t, slot):
                plan = ((9, keep_logits), (X1_ROOT, var_of_x1), (2, eps_times_sum), (4, stats_of_delta),
                        (2, denominator), (5, centre_delta), (2, factor), (DELTA_ROOT, var_of_delta),
                        (5, first_residual), (2, norm_ctx), (7, norm_x1), (5, stats_of_x1))
                for behind, work in plan:
                    if exists(t - behind):
                        work(t - behind, (slot - behind) % 2)
            tile_steps(dve, step)

            dve.wait_ge(logits_kept, NT)
            dve.wait_ge(w_lo, NPIECE)

            def input_lo(i, slot):
                dve.wait_ge(xs_hi, i + 1)
                dve.tensor_tensor(xs_p[:, slot, 1], tile_cols(qc[:, 2:4], i), xs_p[:, slot, 0].bitcast(F32),
                                  ALU.subtract).then_inc(xs_lo, 1)

            input_lo(0, 0)
            for e in range(E):
                dve.memset(iota_e[:, :, e:e + 1], float(e))
            m1, m2, first_e, wgt = (r_m[:, q] for q in range(4))

            def wide(m):
                return m.unsqueeze(2).to_broadcast([P, NT, E])
            linked(dve.tensor_reduce(m1, lg[:], AX_X, ALU.max))
            linked(dve.tensor_tensor(r_a[:], lg[:], wide(m1), ALU.not_equal))
            linked(dve.scalar_tensor_tensor(out=r_b[:], in0=r_a[:], scalar=float(E), in1=iota_e[:], op0=ALU.mult,
                                            op1=ALU.add))
            linked(dve.tensor_reduce(first_e, r_b[:], AX_X, ALU.min))
            linked(dve.tensor_tensor(r_a[:], iota_e[:], wide(first_e), ALU.is_equal))
            linked(dve.scalar_tensor_tensor(out=r_b[:], in0=r_a[:], scalar=-3.0e38, in1=lg[:], op0=ALU.mult,
                                            op1=ALU.add))
            linked(dve.tensor_reduce(m2, r_b[:], AX_X, ALU.max))
            linked(dve.tensor_tensor(first_e, m2, m1, ALU.subtract))
            dve.tensor_copy(m2, first_e).then_inc(gap_ready, 1)
            dve.wait_ge(gap_exped, 1)
            linked(dve.tensor_scalar(wgt, wgt, 1.0, None, ALU.add))
            linked(dve.reciprocal(wgt, wgt))
            dve.tensor_tensor(lg[:], r_a[:], wide(wgt), ALU.mult).then_inc(combine_ready, 1)

            dve.wait_ge(combine_ready, 1)

            def hidden(i, slot, e):
                dve.wait_ge(silu_done, i * E + e + 1)
                col = lg[:, i, e:e + 1] if isinstance(i, int) else \
                    lg[:, bass.ds(i, 1), e:e + 1].rearrange("p o n -> p (o n)")
                dve.scalar_tensor_tensor(out=act[:, slot, e * I:(e + 1) * I], in0=sil[:, e % 2], scalar=col,
                                         in1=gu_ps(e)[:, I:2 * I], op0=ALU.mult, op1=ALU.mult).then_inc(act_ready, 1)

            def hidden_lo(i, q):
                n = min(4, NF - 4 * q)
                dve.wait_ge(actt_hi, i * 3 + q + 1)
                dve.tensor_tensor(actt_p[:, 1, 4 * q:4 * q + n].rearrange("p f n -> p (f n)"), ps[:, 2 + q, 0:n * P],
                                  actt_p[:, 0, 4 * q:4 * q + n].rearrange("p f n -> p (f n)").bitcast(F32),
                                  ALU.subtract).then_inc(actt_lo, 1)

            def finish(i, slot):
                dve.wait_ge(down_done, i + 1)
                if isinstance(i, int):
                    if i >= 2:
                        dve.wait_ge(y_stored[slot], 16 * (i // 2))
                else:
                    dve.wait_ge(y_stored[slot], (i - slot) * 8)
                dve.scalar_tensor_tensor(out=y_out[:, slot], in0=ps[:, 5, 0:D], scalar=tg[:, 1:2], in1=one(x_all, i),
                                         op0=ALU.mult, op1=ALU.add).then_inc(y_ready, 1)

            def expert_tile(i, slot, has_before, has_next):
                if has_next:
                    input_lo(i + 1, 1 - slot)
                for e in range(E):
                    hidden(i, slot, e)
                    if has_before:
                        if 2 <= e < 5:
                            hidden_lo(i - 1, e - 2)
                        if e == 7:
                            finish(i - 1, 1 - slot)
            expert_tile(0, 0, False, True)
            expert_tile(1, 1, True, True)
            with dve.Fori(1, NT // 2) as r:
                expert_tile(r * 2, 0, True, True)
                expert_tile(r * 2 + 1, 1, True, True)
            expert_tile(NT - 1, 0, True, False)
            for q in range(3):
                hidden_lo(NT - 1, q)
            finish(NT - 1, 0)

        @block.scalar
        def _(ac):
            def roots(k):
                ac.wait_ge(var_ready, k + 2)
                ac.activation(rstd[:], var[:], ACT.Sqrt, bias=eps_ln[:, 0:1]).then_inc(std_ready, 1)

            ac.wait_ge(params_loaded, 16 * NPARAM)
            for k in range(2):
                ac.activation(tg[:, k:k + 1], scal[:, k:k + 1], ACT.Tanh).then_inc(gates_ready, 1)
            roots(0)
            for k in range(NBLK):
                for kc in range(KC):
                    ac.wait_ge(hs_transposed, k + 1)
                    if k >= 1:
                        ac.wait_ge(q_projected, G * k)
                    ac.copy(hst_p[:, 0, kc], tps(kc, 0, BT * P)).then_inc(hst_hi, 1)
                for g in range(G):
                    ac.wait_ge(q_projected, G * k + g + 1)
                    ac.activation(qc[:, g, k * BT * P:(k + 1) * BT * P].rearrange("p (h n) -> p h n", h=2),
                                  ps[:, 4 + 2 * (g % 2):6 + 2 * (g % 2), 0:BT * P // 2], ACT.Identity,
                                  bias=bq_sb[:, g:g + 1]).then_inc(q_stored, 1)

            ac.wait_ge(mask_ready, NKT)
            ac.wait_ge(q_stored, G * NBLK)

            def key_hi(g, c, m):
                ac.wait_ge(k_projected, g * 2 + m + 1)
                if not (isinstance(g, int) and g < 2):
                    ac.wait_ge(scored, g * UPC - UPC)
                for h in range(2):
                    ac.activation(kt_p[0:GR, c % 2, 2 * m + h, :], kps(m)[h * GR:(h + 1) * GR], ACT.Identity,
                                  bias=bk_sb[h * GR:(h + 1) * GR, m:m + 1]).then_inc(k_hi, 1)

            def column(tab, n, t, g):
                return tab[0:n, t, g:g + 1] if isinstance(g, int) else tab[0:n, t, bass.ds(g, 1)]

            def expo(b, u, g):
                n, t = KEYS[(u % UPC) // 2], (u % UPC) // 2
                U = b * UPB + u
                ac.wait_ge(scored, U + 1)
                if not (isinstance(b, int) and b * UPB + u < NE):
                    ac.wait_ge(pv_done, U - (NE - 1))
                ac.nop(nofuse=True)
                ac.activation(ex[0:n, u % NE], sps(u)[0:n], ACT.Exp, bias=column(m_bias, n, t, g),
                              scale=column(m_scale, n, t, g)).then_inc(exped, 1)

            def save_ctx(b):
                ac.wait_ge(pv_done, b * UPB + UPB)
                ac.wait_ge(q_built, b * G + G)
                dst = qc[:, :, b * S:(b + 1) * S] if isinstance(b, int) else qc[:, :, bass.ds(b * S, S)]
                ac.copy(dst, ctx_ps.rearrange("p (g s) -> p g s", g=G)).then_inc(ctx_saved, 1)

            def attend(b, first_batch, last_batch):
                for u in range(UPB):
                    c, v = divmod(u, UPC)
                    g = b * CPB + c
                    expo(b, u, g)
                    if v < 2 and not (last_batch and c == CPB - 1):
                        key_hi(g + 1, c + 1, v)
                    if u == LAG - 1 and not first_batch:
                        save_ctx(b - 1)
            key_hi(0, 0, 0)
            key_hi(0, 0, 1)
            attend(0, True, False)
            with ac.Fori(1, B - 1) as b:
                attend(b, False, False)
            attend(B - 1, False, True)
            save_ctx(B - 1)

            def stage(i, slot):
                used(ac, stage_transposed, i - 1)
                if isinstance(i, int):
                    ac.wait_ge(ctx_saved, B)
                ac.copy(stg[:, slot], tile_cols(qc, i)).then_inc(staged, 1)

            def transposed_ctx(i, slot):
                ac.wait_ge(ctxn_transposed, i + 1)
                used(ac, o_projected, i - 1)
                ac.copy(ctxt[:, slot].rearrange("p k n -> p (k n)"), ps[:, 2 + slot, 0:D]).then_inc(ctxt_ready, 1)

            def scaled_delta(i, slot):
                ac.wait_ge(o_projected, i + 1)
                used(ac, zed_ready, i - 1)
                ac.activation(dlt[:, slot], ps[:, 4 + slot, 0:D], ACT.Copy, scale=rsc[:, 0:1]
                              ).then_inc(delta_ready, 1)

            def transposed_xn(i, slot):
                ac.wait_ge(xn_transposed, i + 1)
                used(ac, logits_done, i - 1)
                src = ps[:, 6 + slot, 0:D].rearrange("p (k n) -> p k n", k=KC)
                ac.copy(xts[:, slot], src).then_inc(xts_ready, 1)
                ac.copy(tile_cols(qc[:, 2:4], i), src).then_inc(xt_kept, 1)

            def split_high(k):
                if isinstance(k, int):
                    ac.wait_ge(w_loaded[k * LOADS // NPIECE], 16)
                ac.copy(piece(0, k), one(w_in, k)).then_inc(w_hi, 1)

            def step(t, slot):
                if exists(t):
                    stage(t, slot)
                if exists(t - 3):
                    scaled_delta(t - 3, 1 - slot)
                if exists(t - 2):
                    transposed_ctx(t - 2, slot)
                if exists(t - 7):
                    transposed_xn(t - 7, 1 - slot)
                k = piece_of_step(t, slot)
                if k is not None:
                    if not isinstance(k, int):
                        for n in range(LOADS):
                            ac.wait_ge(w_loaded[n], 16)
                    split_high(k)
            tile_steps(ac, step)
            ac.wait_ge(w_lo, NPIECE)

            ac.wait_ge(xt_kept, NT)

            def input_hi(i, slot):
                if not (isinstance(i, int) and i < 2):
                    ac.wait_ge(gu_done, i * E - E)
                src = qc[:, 2:4, i * P:(i + 1) * P] if isinstance(i, int) else qc[:, 2:4, bass.ds(i * P, P)]
                ac.copy(xs_p[:, slot, 0], src).then_inc(xs_hi, 1)

            def silu(i, slot, e):
                ac.wait_ge(gu_done, i * E + e + 1)
                if not (isinstance(i, int) and i == 0 and e < 2):
                    ac.wait_ge(act_ready, i * E + e - 1)
                ac.activation(sil[:, e % 2], gu_ps(e)[:, 0:I], ACT.Silu).then_inc(silu_done, 1)

            def hidden_hi(i, q):
                n = min(4, NF - 4 * q)
                ac.wait_ge(act_transposed, i * 3 + q + 1)
                if not (isinstance(i, int) and i == 0):
                    ac.wait_ge(down_done, i)
                ac.copy(actt_p[:, 0, 4 * q:4 * q + n].rearrange("p f n -> p (f n)"), ps[:, 2 + q, 0:n * P]
                        ).then_inc(actt_hi, 1)

            def expert_tile(i, slot, has_before, has_next):
                if has_next:
                    input_hi(i + 1, 1 - slot)
                for e in range(E):
                    silu(i, slot, e)
                    if has_before and 2 <= e < 5:
                        hidden_hi(i - 1, e - 2)
            input_hi(0, 0)
            ac.wait_ge(gap_ready, 1)
            ac.activation(r_m[:, 3], r_m[:, 1], ACT.Exp).then_inc(gap_exped, 1)
            expert_tile(0, 0, False, True)
            expert_tile(1, 1, True, True)
            with ac.Fori(1, NT // 2) as r:
                expert_tile(r * 2, 0, True, True)
                expert_tile(r * 2 + 1, 1, True, True)
            expert_tile(NT - 1, 0, True, False)
            for q in range(3):
                hidden_hi(NT - 1, q)

        @block.tensor
        def _(pe):
            def parts(dst, lhs, rhs, rounds):
                last = None
                todo = [(k, a, b) for k in range(rounds) for a, b in ((0, 0), (0, 1), (1, 0))]
                for q, (k, a, b) in enumerate(todo):
                    last = pe.matmul(dst, lhs(a, k), rhs(b, k), start=q == 0, stop=q == len(todo) - 1)
                return last

            pe.wait_ge(consts_made, 1)
            for k in range(NBLK):
                if k >= 1:
                    pe.wait_ge(hst_lo, KC * k)
                for j in range(BT):
                    pe.wait_ge(hs_ready, BT * k + j + 1)
                    for kc in range(KC):
                        last = pe.transpose(tps(kc, j * P, P), hs[:, j, kc * P:(kc + 1) * P], ident[:])
                last.then_inc(hs_transposed, 1)
                pe.wait_ge(hst_lo, KC * (k + 1))
                pe.wait_ge(wq_split, 2 + 2 * KC)
                for g in range(G):
                    n = G * k + g
                    if n >= 2:
                        pe.wait_ge(q_stored, n - 1)
                    for half in range(2):
                        w = BT * P // 2
                        last = parts(qps(g, half),
                                     lambda p, kc: wq_p[:, p, kc, g].rearrange("p t c -> p (t c)"),
                                     lambda p, kc: hst_p[:, p, kc, half * w:(half + 1) * w], KC)
                    last.then_inc(q_projected, 1)

            pe.wait_ge(w_split, 4)
            pe.wait_ge(pads_set, 4)
            pe.wait_ge(q_stored, G * NBLK)
            pe.matmul(ps[:, 3, :], zeros[:, 0:P], zeros[:], start=True, stop=True).then_inc(ctx_cleared, 1)

            def project_keys(g, c, m):
                pe.wait_ge(at_split, g * 2 + 2)
                if not (isinstance(g, int) and g < 1):
                    pe.wait_ge(k_lo, g * G - G + 2 * m + 2)
                s = c % 2
                parts(kps(m), lambda p, kc: wk_p[:, p, kc, m * P:(m + 1) * P], lambda p, kc: at_p[:, s, p, kc, :],
                      KC).then_inc(k_projected, 1)

            def project_values(g, c, t):
                if not (isinstance(g, int) and g * NKT + t < 1):
                    pe.wait_ge(v_ready, g * NKT + t)
                s, o, n = c % 2, KOFF[t], KEYS[t]
                parts(vps[0:n], lambda p, kc: at_p[:, s, p, kc, o:o + n], lambda p, kc: wv_p[:, p, kc, :],
                      KC).then_inc(v_projected, 1)

            def scores(b, u, g):
                v = u % UPC
                t, half = v // 2, v % 2
                o, n = KOFF[t], KEYS[t]
                U = b * UPB + u
                if not (isinstance(b, int) and b == 0 and u < 2):
                    pe.wait_ge(exped, U - 1)
                if t == 0:
                    pe.wait_ge(k_lo, g * G + 2 * half + 2)
                if u == 0:
                    pe.wait_ge(q_built, b * G + G)
                last = None
                for h in range(2):
                    grp = 2 * half + h
                    for part in range(2):
                        q = qbd[:, b % 2, part, grp] if isinstance(b, int) else \
                            qbd[:, bass.ds(b % 2, 1), part, grp].rearrange("p o h s -> p (o h) s")
                        last = pe.matmul(sps(u)[0:n, h], kt_p[:, (u // UPC) % 2, grp, o:o + n],
                                         q, start=part == 0, stop=part == 1)
                last.then_inc(scored, 1)

            def weigh_values(b, u):
                v = u % UPC
                c, t, half = u // UPC, v // 2, v % 2
                n = KEYS[t]
                U = b * UPB + u
                pe.wait_ge(clipped, U + 1)
                if half == 0:
                    pe.wait_ge(v_ready, (b * CPB + c) * NKT + t + 1)
                if u == 0 and not (isinstance(b, int) and b == 0):
                    pe.wait_ge(ctx_saved, b)
                last = None
                for q in range(2 * HG):
                    h = 2 * HG * half + q
                    s, j = h // HG, h % HG
                    last = pe.matmul(ctx_ps[32 * j:32 * j + VW, s * S:(s + 1) * S], v_sb[0:n, c % 2, t, h, :],
                                     ex[0:n, u % NE, q // HG, j * S:(j + 1) * S],
                                     start=u == 0 and s == 0, stop=u >= UPB - 2 and s == 2 * half + 1,
                                     skip_group_check=True)
                last.then_inc(pv_done, 1)

            def attend(b, first_batch, last_batch):
                for u in range(UPB):
                    c, v = divmod(u, UPC)
                    g = b * CPB + c
                    more = not (last_batch and c == CPB - 1)
                    scores(b, u, g)
                    if v < 2 and more:
                        project_keys(g + 1, c + 1, v)
                    if v in (2, 5) and more:
                        project_values(g + 1, c + 1, 0 if v == 2 else 2)
                    if u % 2 == 1:
                        for w in (u - LAG, u - LAG + 1):
                            if w >= 0:
                                weigh_values(b, w)
                            elif not first_batch:
                                weigh_values(b - 1, w + UPB)
                    if v == 3 and more:
                        project_values(g + 1, c + 1, 1)
            project_keys(0, 0, 0)
            project_keys(0, 0, 1)
            for t in range(NKT):
                project_values(0, 0, t)
            attend(0, True, False)
            with pe.Fori(1, B - 1) as b:
                attend(b, False, False)
            attend(B - 1, False, True)
            for u in range(UPB - LAG + 1, UPB):
                weigh_values(B - 1, u)

            pe.wait_ge(params_loaded, 16 * NPARAM)

            def transpose_stage(i, slot):
                pe.wait_ge(staged, i + 1)
                used(pe, ctx_normed, i - 1)
                for g in range(G):
                    last = pe.transpose(ps[:, slot, g * P:(g + 1) * P], stg[:, slot, g], ident[:])
                last.then_inc(stage_transposed, 1)

            def transpose_ctx(i, slot):
                pe.wait_ge(ctx_normed, i + 1)
                used(pe, ctxt_ready, i - 1)
                for kc in range(KC):
                    last = pe.transpose(ps[:, 2 + slot, kc * P:(kc + 1) * P], ctxn[:, slot, kc * P:(kc + 1) * P],
                                        ident[:])
                last.then_inc(ctxn_transposed, 1)

            def project_ctx(i, slot):
                pe.wait_ge(ctxt_ready, i + 1)
                used(pe, delta_ready, i - 1)
                dst = ps[:, 4 + slot, 0:D]
                for kc in range(KC):
                    pe.matmul(dst, ctxt[:, slot, kc], wo_sb[:, kc], start=kc == 0, stop=False)
                pe.matmul(dst, ident[:], bo_sb[:], start=False, stop=True).then_inc(o_projected, 1)

            def transpose_xn(i, slot):
                pe.wait_ge(xn_ready, i + 1)
                used(pe, logits_kept, i - 1)
                for kc in range(KC):
                    last = pe.transpose(ps[:, 6 + slot, kc * P:(kc + 1) * P], xn[:, slot, kc * P:(kc + 1) * P],
                                        ident[:])
                last.then_inc(xn_transposed, 1)

            def logits(i, slot):
                pe.wait_ge(xts_ready, i + 1)
                pe.wait_ge(xt_kept, i + 1)
                for kc in range(KC):
                    last = pe.matmul(ps[:, 6 + slot, D:D + E], xts[:, slot, kc], rw_sb[:, kc], start=kc == 0,
                                     stop=kc == KC - 1)
                last.then_inc(logits_done, 1)

            def step(t, slot):
                plan = ((1, transpose_stage), (3, project_ctx), (8, logits), (2, transpose_ctx), (7, transpose_xn))
                for behind, work in plan:
                    if exists(t - behind):
                        work(t - behind, (slot - behind) % 2)
            tile_steps(pe, step)

            pe.wait_ge(xt_kept, NT)
            pe.wait_ge(logits_kept, NT)
            pe.wait_ge(w_lo, NPIECE)

            def gate_up(i, slot, e):
                if not (isinstance(i, int) and i == 0 and e < 4):
                    pe.wait_ge(act_ready, i * E + e - 3)
                parts(gu_ps(e)[:, 0:2 * I], lambda p, kc: xs_p[:, slot, p, kc, :],
                      lambda p, kc: gu_w(p, kc, e), KC).then_inc(gu_done, 1)

            def transpose_hidden(i, slot, q):
                if q == 0:
                    pe.wait_ge(act_ready, i * E + E)
                if not (isinstance(i, int) and i == 0):
                    pe.wait_ge(actt_lo, i * 3 - 3 + q + 1)
                n = min(4, NF - 4 * q)
                for f in range(4 * q, 4 * q + n):
                    last = pe.transpose(ps[:, 2 + q, (f % 4) * P:(f % 4 + 1) * P], act[:, slot, f * P:(f + 1) * P],
                                        ident[:])
                last.then_inc(act_transposed, 1)

            def down_proj(i):
                pe.wait_ge(actt_lo, i * 3 + 3)
                if not (isinstance(i, int) and i == 0):
                    pe.wait_ge(y_ready, i)
                parts(ps[:, 5, 0:D], lambda p, f: actt_p[:, p, f, :], dn_w,
                      NF).then_inc(down_done, 1)

            def expert_tile(i, slot, has_before):
                pe.wait_ge(xs_lo, i + 1)
                for e in range(E):
                    gate_up(i, slot, e)
                    if has_before and 1 <= e < 4:
                        transpose_hidden(i - 1, 1 - slot, e - 1)
                    if has_before and e == 6:
                        down_proj(i - 1)
            expert_tile(0, 0, False)
            expert_tile(1, 1, True)
            with pe.Fori(1, NT // 2) as r:
                expert_tile(r * 2, 0, True)
                expert_tile(r * 2 + 1, 1, True)
            expert_tile(NT - 1, 0, True)
            for q in range(3):
                transpose_hidden(NT - 1, 0, q)
            down_proj(NT - 1)


def kernel(x, ctx_2048, mask_BxS2_ik0, g_xattn, g_ffn, L0_xattn_Wq, L0_xattn_bq, L0_xattn_Wk, L0_xattn_bk,
           L0_xattn_Wv, L0_xattn_bv, L0_xattn_Wo, L0_xattn_bo, L0_xattn_ln_gamma, L0_xattn_ln_beta,
           L0_xattn_residual_scale, L0_ffn_router_w, L0_ffn_gate_w, L0_ffn_up_w, L0_ffn_down_w):
    import concourse.bacc as bacc
    from concourse.bass_utils import run_bass_kernel_spmd

    def lay(a):
        return np.ascontiguousarray(a)

    def weight(w):
        w = np.asarray(w)
        return lay(w.T.reshape(KC, P, w.shape[0]).transpose(1, 0, 2))

    def experts_in(w):
        return np.asarray(w).transpose(2, 0, 1).reshape(KC, P, E, I).transpose(1, 0, 2, 3)

    gate_up = np.concatenate([experts_in(L0_ffn_gate_w), experts_in(L0_ffn_up_w)], axis=3)
    down = np.asarray(L0_ffn_down_w).transpose(0, 2, 1).reshape(NF, P, D).transpose(1, 0, 2)
    bq = np.asarray(L0_xattn_bq).reshape(G, GR)
    data = {
        "x": lay(np.asarray(x).reshape(TOK, D)),
        "ctx_t": lay(np.asarray(ctx_2048).reshape(NCH, CHUNK, KC, P).transpose(0, 3, 2, 1)),
        "mask_t": lay(np.asarray(mask_BxS2_ik0).reshape(NCH, CHUNK).T),
        "g_xattn": lay(np.asarray(g_xattn).reshape(1)),
        "g_ffn": lay(np.asarray(g_ffn).reshape(1)),
        "wq": weight(L0_xattn_Wq),
        "bq": lay(np.concatenate([bq, bq], axis=1).T),
        "wk": weight(L0_xattn_Wk),
        "bk": lay(np.asarray(L0_xattn_bk).reshape(KC, P).T),
        "wv": weight(L0_xattn_Wv),
        "bv": lay(L0_xattn_bv),
        "wo": weight(L0_xattn_Wo),
        "bo": lay(L0_xattn_bo),
        "gamma": lay(L0_xattn_ln_gamma),
        "beta": lay(L0_xattn_ln_beta),
        "rs": lay(np.asarray(L0_xattn_residual_scale).reshape(1)),
        "router": weight(L0_ffn_router_w),
        "w_ffn": lay(np.concatenate([gate_up.reshape(P, -1), down.reshape(P, -1)], axis=1).reshape(P, NPIECE, PIECE)),
    }
    nc = bacc.Bacc("TRN2", target_bir_lowering=False, num_devices=1)
    args = [nc.dram_tensor(name, a.shape, mybir.dt.from_np(a.dtype), kind="ExternalInput").ap()
            for name, a in data.items()]
    out = nc.dram_tensor("out", (TOK, D), F32, kind="ExternalOutput").ap()
    build(nc, *args, out)
    r = run_bass_kernel_spmd(nc, [data], core_ids=[0])
    return r.results[0]["out"].reshape(B, S, D)
```

```python
from contextlib import ExitStack

import numpy as np

import concourse.bass as bass
from concourse import mybir

F32 = mybir.dt.float32
F32R = mybir.dt.float32r
I32 = mybir.dt.int32
ALU = mybir.AluOpType
ACT = mybir.ActivationFunctionType
AX_X = mybir.AxisListType.X

P = 128
B, S, T, D = 32, 100, 1444, 256
H, HD = 16, 16
E, I = 8, 176
EPS_LN = 1e-5
EPS_PROBS = 1e-8
SCORE_CLIP = 50.0
RES_SCALE_MAX = 0.3
EXP_HI = float(np.exp(np.float64(SCORE_CLIP)))
EXP_LO = float(np.exp(np.float64(-SCORE_CLIP)))

KC = D // P
TOK = B * S
NT = TOK // P
BT = 5
NBLK = NT // BT

CPB = 4
CHUNK = T // CPB
CW = CHUNK + 1
KEYS = [121, 120, 120]
KOFF = [0, 121, 241]
NKT = len(KEYS)
G, HG = 4, 4
GR = HG * HD
UPC = 2 * NKT
UPB = UPC * CPB
NCH = B * CPB
NE = 4
PVG = 2
VALUES_AT = {2: (0, False), 3: (1, True), 5: (2, False)}
VW = HD + 1

NPARAM = 10 + 3 + NKT
NF = E * I // P
PIECE = 4 * I
NGU = KC * E * 2 * I // PIECE
NDN = NF * D // PIECE
NPIECE = NGU + NDN
LOADS = 4
DEPTH = 10
DELTA_ROOT, X1_ROOT = 5, 7
FIRST_PIECE = 3


def build(nc, x, ctx_t, mask_t, g_xattn, g_ffn, wq, bq, wk, bk, wv, bv, wo, bo, gamma, beta, rs, router,
          w_ffn, out):
    top = ExitStack()

    def sem(name):
        return top.enter_context(nc.semaphore(name))

    def sb(stack, name, shape, dt=F32):
        return stack.enter_context(nc.sbuf_tensor(name, shape, dt))

    with top:
        ps = top.enter_context(nc.psum_tensor("ps", [P, 8, 512], F32))
        psf = ps[:].rearrange("p b n -> p (b n)")
        x_all = sb(top, "x_all", [P, NT, D])
        qc = sb(top, "qc", [P, G, TOK])
        ident = sb(top, "ident", [P, P])
        wo_sb = sb(top, "wo_sb", [P, KC, D])
        gam = sb(top, "gam", [P, D])
        bet = sb(top, "bet", [P, D])
        bo_sb = sb(top, "bo_sb", [P, D])
        bv_sb = sb(top, "bv_sb", [P, D])
        bq_sb = sb(top, "bq_sb", [P, G])
        bk_sb = sb(top, "bk_sb", [P, KC])
        rw_sb = sb(top, "rw_sb", [P, KC, E])
        scal = sb(top, "scal", [P, 3])
        tg = sb(top, "tg", [P, 2])
        rsc = sb(top, "rsc", [P, 1])
        eps_ln = sb(top, "eps_ln", [P, 1])
        minus_half = sb(top, "minus_half", [P, 1])
        lg = sb(top, "lg", [P, NT, E])

        params_loaded = sem("params_loaded")
        wq_loaded = sem("wq_loaded")
        x_loaded = [sem(f"x_loaded{k}") for k in range(NBLK)]
        consts_made = sem("consts_made")
        chain = sem("chain")
        gates_ready = sem("gates_ready")
        gates_applied = sem("gates_applied")
        rsc_ready = sem("rsc_ready")


        attn = ExitStack()
        mask_i = sb(attn, "mask_i", [P, NKT, NCH], I32)
        m_scale = sb(attn, "m_scale", [P, NKT, NCH])
        m_bias = sb(attn, "m_bias", [P, NKT, NCH])
        w_raw = sb(attn, "w_raw", [P, KC, D])
        w_raw2 = sb(attn, "w_raw2", [P, KC, D])
        w_raw3 = sb(attn, "w_raw3", [P, KC, D])
        wk_p = sb(attn, "wk_p", [P, 2, KC, D], F32R)
        wv_p = sb(attn, "wv_p", [P, 2, KC, D], F32R)
        head_mask = sb(attn, "head_mask", [P, HG, S])
        zeros = sb(attn, "zeros", [P, 512])

        at_raw = sb(attn, "at_raw", [P, 2, KC, CHUNK])
        at_p = sb(attn, "at_p", [P, 2, 2, KC, CW], F32R)
        qbd = sb(attn, "qbd", [P, 2, 2, G, HG, S], F32R)
        qprod = sb(attn, "qprod", [P, 2, HG, S])

        first = ExitStack()
        wq_p = sb(first, "wq_p", [P, 2, KC, G, 2, GR], F32R)
        hs = sb(first, "hs", [P, 2, BT, D])
        hst_p = sb(first, "hst_p", [P, 2, 2, KC, BT * P], F32R)
        stats = sb(first, "stats", [P, NT, 6])
        mv_in = sb(first, "mv_in", [P, NT, 2])
        var_in = sb(first, "var_in", [P, NT])
        rstd = sb(first, "rstd", [P, NT])
        first.close()

        kt_p = sb(attn, "kt_p", [P, 2, G, CW], F32R)
        v_sb = sb(attn, "v_sb", [P, 2, NKT, H, VW])
        ex = sb(attn, "ex", [P, NE, 2, HG * S])
        attn.close()

        ffn = ExitStack()
        xn = sb(ffn, "xn", [P, 2, D])
        xts = sb(ffn, "xts", [P, 2, KC, P])
        w_p = sb(ffn, "w_p", [P, 2, NPIECE, PIECE], F32R)
        outp = ExitStack()
        w_in = sb(outp, "w_in", [P, NPIECE, PIECE])
        stg = sb(outp, "stg", [P, 2, G, P])
        ctxn = sb(outp, "ctxn", [P, 2, D])
        ctxt = sb(outp, "ctxt", [P, 2, KC, P])
        dlt = sb(outp, "dlt", [P, 2, D])
        zed = sb(outp, "zed", [P, 2, D])
        den = sb(outp, "den", [P, 3, 2, H])
        st_d = sb(outp, "st_d", [P, 2, 6])
        st_x = sb(outp, "st_x", [P, 2, 6])
        mv = sb(outp, "mv", [P, 2, 2, 2])
        var_eps = sb(outp, "var_eps", [P, 2, 2])
        rstds = sb(outp, "rstds", [P, 2, 2])
        outp.close()
        actt_p = sb(ffn, "actt_p", [P, 2, NF, P], F32R)
        act = sb(ffn, "act", [P, 2, NF * P])
        xs_p = sb(ffn, "xs_p", [P, 2, 2, KC, P], F32R)
        sil = sb(ffn, "sil", [P, 3, I])
        y_out = sb(ffn, "y_out", [P, 2, D])
        r_a = sb(ffn, "r_a", [P, NT, E])
        r_b = sb(ffn, "r_b", [P, NT, E])
        iota_e = sb(ffn, "iota_e", [P, NT, E])
        r_m = sb(ffn, "r_m", [P, 4, NT])
        ffn.close()

        x_stats = sem("x_stats")
        x_var = sem("x_var")
        x_var_eps = sem("x_var_eps")
        x_rstd = sem("x_rstd")
        eps_set = sem("eps_set")
        hs_ready = sem("hs_ready")
        hs_transposed = sem("hs_transposed")
        hst_hi = sem("hst_hi")
        hst_lo = sem("hst_lo")
        wq_split = sem("wq_split")
        q_projected = sem("q_projected")
        q_stored = sem("q_stored")
        w_split = sem("w_split")
        mask_ready = sem("mask_ready")
        pads_set = sem("pads_set")
        at_loaded = [sem("at_loaded0"), sem("at_loaded1")]
        at_split = sem("at_split")
        k_projected = sem("k_projected")
        k_hi = sem("k_hi")
        k_lo = sem("k_lo")
        v_projected = sem("v_projected")
        v_ready = sem("v_ready")
        q_built = sem("q_built")
        pool_chain = sem("pool_chain")
        scored = sem("scored")
        exped = sem("exped")
        clipped = sem("clipped")
        pv_done = sem("pv_done")
        ctx_cleared = sem("ctx_cleared")
        ctx_saved = sem("ctx_saved")
        staged = sem("staged")
        stage_transposed = sem("stage_transposed")
        eps_sums = sem("eps_sums")
        den_ready = sem("den_ready")
        recip_ready = sem("recip_ready")
        ctx_normed = sem("ctx_normed")
        ctxn_transposed = sem("ctxn_transposed")
        ctxt_ready = sem("ctxt_ready")
        o_projected = sem("o_projected")
        delta_ready = sem("delta_ready")
        delta_stats = sem("delta_stats")
        delta_var = sem("delta_var")
        zed_ready = sem("zed_ready")
        x1_ready = sem("x1_ready")
        x1_stats = sem("x1_stats")
        x1_var = sem("x1_var")
        vars_widened = sem("vars_widened")
        roots_ready = sem("roots_ready")
        xn_ready = sem("xn_ready")
        xn_transposed = sem("xn_transposed")
        xts_ready = sem("xts_ready")
        xt_kept = sem("xt_kept")
        logits_done = sem("logits_done")
        logits_kept = sem("logits_kept")
        beta_added = sem("beta_added")
        w_loaded = [sem(f"w_loaded{k}") for k in range(LOADS)]
        w_hi = sem("w_hi")
        w_lo = sem("w_lo")
        gap_ready = sem("gap_ready")
        gap_exped = sem("gap_exped")
        combine_ready = sem("combine_ready")
        xs_hi = sem("xs_hi")
        xs_lo = sem("xs_lo")
        gu_done = sem("gu_done")
        silu_done = sem("silu_done")
        act_ready = sem("act_ready")
        act_transposed = sem("act_transposed")
        actt_hi = sem("actt_hi")
        actt_lo = sem("actt_lo")
        down_done = sem("down_done")
        y_ready = sem("y_ready")
        y_stored = [sem("y_stored0"), sem("y_stored1")]

        def tps(kc, lo, n):
            return psf[:, kc * 1024 + lo:kc * 1024 + lo + n]

        def qps(g, half):
            return ps[:, 4 + 2 * (g % 2) + half, 0:BT * P // 2]

        def kps(m):
            return ps[:, m, 0:CW]
        vps = ps[:, 2, 0:D]
        ctx_ps = ps[:, 3, 0:G * S]

        def sps(u):
            return ps[:, 4 + 2 * (u % 2):6 + 2 * (u % 2), 0:HG * S]

        def gu_ps(e):
            return ps[:, (0, 1, 6, 7)[e % 4]]

        def used(eng, semaphore, value):
            if not isinstance(value, int) or value > 0:
                eng.wait_ge(semaphore, value)

        block = top.enter_context(nc.Block())

        def gu_w(p, kc, e):
            return w_p[:, p, 0:NGU].rearrange("p n w -> p (n w)")[:, (kc * E + e) * 2 * I:(kc * E + e + 1) * 2 * I]

        def dn_w(p, f):
            return w_p[:, p, NGU:NPIECE].rearrange("p n w -> p (n w)")[:, f * D:(f + 1) * D]

        def tile_steps(eng, step):
            start = DEPTH + 2
            stop = start + (NT - start) // 2 * 2
            for t in range(start):
                step(t, t % 2)
            with eng.Fori(0, (stop - start) // 2) as r:
                step(r * 2 + start, start % 2)
                step(r * 2 + start + 1, (start + 1) % 2)
            for t in range(stop, NT + DEPTH):
                step(t, t % 2)

        def exists(i):
            return not isinstance(i, int) or 0 <= i < NT

        def tile_cols(ap, i):
            return ap[:, :, i * P:(i + 1) * P] if isinstance(i, int) else ap[:, :, bass.ds(i * P, P)]

        def one(ap, i):
            return ap[:, i] if isinstance(i, int) else ap[:, bass.ds(i, 1)].rearrange("p o n -> p (o n)")

        def piece(part, k):
            return one(w_p[:, part], k)

        def piece_of_step(t, slot):
            if slot != FIRST_PIECE % 2:
                return None
            if not isinstance(t, int):
                return ((t - FIRST_PIECE) // 2)
            k = (t - FIRST_PIECE) // 2
            return k if 0 <= k < NPIECE else None

        @block.sync
        def _(sp):
            def load_x(k):
                sp.dma_start(x_all[:, k * BT:(k + 1) * BT, :],
                             x.rearrange("(n p) d -> p n d", p=P)[:, k * BT:(k + 1) * BT, :]).then_inc(x_loaded[k], 16)
            load_x(0)
            load_x(1)
            sp.dma_start(w_raw[:], wq).then_inc(wq_loaded, 16)
            load_x(2)
            for dst, src in ((w_raw2, wk), (w_raw3, wv)):
                sp.dma_start(dst[:], src).then_inc(params_loaded, 16)
            load_x(3)
            load_x(4)
            for t in range(NKT):
                sp.dma_start(mask_i[0:KEYS[t], t, :], mask_t[KOFF[t]:KOFF[t] + KEYS[t], :]).then_inc(params_loaded, 16)

            def load_chunk(b, c):
                sp.dma_start(at_raw[:, c % 2], ctx_t[b * CPB + c] if isinstance(b, int)
                             else ctx_t[bass.ds(b * CPB + c, 1)].rearrange("o p k n -> (o p) k n")
                             ).then_inc(at_loaded[c % 2], 16)
            for c in range(CPB):
                if c >= 2:
                    sp.wait_ge(at_split, 2 * (c - 1))
                load_chunk(0, c)
            with sp.Fori(1, B) as b:
                for c in range(CPB):
                    sp.wait_ge(at_split, b * 2 * CPB + 2 * (c - 1))
                    load_chunk(b, c)
            sp.wait_ge(ctx_saved, B)
            for k in range(LOADS):
                n = NPIECE // LOADS
                sp.dma_start(w_in[:, k * n:(k + 1) * n], w_ffn[:, k * n:(k + 1) * n]).then_inc(w_loaded[k], 16)

            def store(i, slot):
                sp.wait_ge(y_ready, i + 1)
                dst = out[i * P:(i + 1) * P, :] if isinstance(i, int) else out[bass.ds(i * P, P), :]
                sp.dma_start(dst, y_out[:, slot, :]).then_inc(y_stored[slot], 16)
            with sp.Fori(0, NT // 2) as r:
                store(r * 2, 0)
                store(r * 2 + 1, 1)
            store(NT - 1, 0)
            sp.wait_ge(y_stored[0], 16 * (NT // 2 + 1))
            sp.wait_ge(y_stored[1], 16 * (NT // 2))

        @block.gpsimd
        def _(pool):
            nc.gpsimd.memset(ident[:], 1.0).then_inc(pool_chain, 1)
            nc.gpsimd.memset(head_mask[:], 1.0).then_inc(pool_chain, 1)
            pool.wait_ge(pool_chain, 2)
            nc.gpsimd.affine_select(out=ident[:], in_=ident[:], compare_op=ALU.is_equal, fill=0.0, base=0,
                                    pattern=[[-1, P]], channel_multiplier=1).then_inc(consts_made, 1)
            for half in range(2):
                w = head_mask[half * GR:(half + 1) * GR]
                nc.gpsimd.affine_select(out=w, in_=w, compare_op=ALU.is_ge, fill=0.0, base=0,
                                        pattern=[[-HD, HG], [0, S]], channel_multiplier=1).then_inc(pool_chain, 1)
                pool.wait_ge(pool_chain, 3 + 2 * half)
                nc.gpsimd.affine_select(out=w, in_=w, compare_op=ALU.is_ge, fill=0.0, base=HD - 1,
                                        pattern=[[HD, HG], [0, S]], channel_multiplier=-1).then_inc(pool_chain, 1)
            pool.wait_ge(pool_chain, 6)
            pool.wait_ge(eps_set, 2)
            for k in range(NBLK):
                tiles = slice(k * BT, (k + 1) * BT)
                pool.wait_ge(x_var, (k + 1) * BT)
                nc.gpsimd.tensor_tensor(var_in[:, tiles], mv_in[:, tiles, 1], eps_ln[:].to_broadcast([P, BT]), ALU.add
                                        ).then_inc(x_var_eps, 1)
                pool.wait_ge(x_var_eps, k + 1)
                nc.gpsimd.tensor_tensor(rstd[:, tiles], var_in[:, tiles], minus_half[:].to_broadcast([P, BT]), ALU.pow
                                        ).then_inc(x_rstd, 1)
            BASE = 6

            def build_q(b, slot):
                for g in range(G):
                    k = b * (2 * G) + BASE + 2 * g
                    q = qc[:, g, b * S:(b + 1) * S] if isinstance(b, int) else qc[:, g, bass.ds(b * S, S)]
                    hi = qbd[:, slot, 0, g] if isinstance(b, int) else \
                        qbd[:, bass.ds(slot, 1), 0, g].rearrange("p o h s -> p (o h) s")
                    lo = qbd[:, slot, 1, g] if isinstance(b, int) else \
                        qbd[:, bass.ds(slot, 1), 1, g].rearrange("p o h s -> p (o h) s")
                    prod = qprod[:, g % 2]
                    nc.gpsimd.tensor_tensor(prod, q.unsqueeze(1).to_broadcast([P, HG, S]), head_mask[:],
                                            ALU.mult).then_inc(pool_chain, 1)
                    pool.wait_ge(pool_chain, k + 1)
                    nc.gpsimd.tensor_copy(hi, prod).then_inc(pool_chain, 1)
                    pool.wait_ge(pool_chain, k + 2)
                    nc.gpsimd.tensor_tensor(lo, prod, hi.bitcast(F32), ALU.subtract).then_inc(q_built, 1)

            pool.wait_ge(q_stored, G)
            build_q(0, 0)
            build_q(1, 1)
            pool.wait_ge(gates_applied, 2)
            pool.wait_ge(hs_ready, NT)
            with pool.Fori(0, NT) as i:
                nc.gpsimd.tensor_tensor(one(x_all, i), one(x_all, i), bet[:], ALU.add).then_inc(beta_added, 1)
            with pool.Fori(2, B) as b:
                pool.wait_ge(q_stored, G * NBLK)
                pool.wait_ge(scored, b * UPB - UPB)
                build_q(b, b % 2)

            def roots(t, slot):
                lo = 0 if exists(t - DELTA_ROOT) else 1
                hi = 2 if exists(t - X1_ROOT) else 1
                if lo >= hi:
                    return
                if lo == 0:
                    pool.wait_ge(delta_var, t - DELTA_ROOT + 1)
                    used(pool, x1_ready, t - DELTA_ROOT - 1)
                if hi == 2:
                    pool.wait_ge(x1_var, t - X1_ROOT + 1)
                    used(pool, xn_ready, t - X1_ROOT - 1)
                nc.gpsimd.tensor_tensor(var_eps[:, slot, lo:hi], mv[:, slot, lo:hi, 1],
                                        eps_ln[:].to_broadcast([P, hi - lo]), ALU.add).then_inc(vars_widened, 1)
                pool.wait_ge(vars_widened, t - DELTA_ROOT + 1)
                nc.gpsimd.tensor_tensor(rstds[:, slot, lo:hi], var_eps[:, slot, lo:hi],
                                        minus_half[:].to_broadcast([P, hi - lo]), ALU.pow).then_inc(roots_ready, 1)

            def split_low(k):
                pool.wait_ge(w_hi, k + 1)
                nc.gpsimd.tensor_tensor(piece(1, k), one(w_in, k), piece(0, k).bitcast(F32),
                                        ALU.subtract).then_inc(w_lo, 1)

            def step(t, slot):
                roots(t, (slot - DELTA_ROOT) % 2)
                k = piece_of_step(t, slot)
                if k is not None:
                    split_low(k)
            pool.wait_ge(ctx_saved, B)
            tile_steps(pool, step)

        @block.vector
        def _(dve):
            n_chain = [0]

            def linked(ins):
                n_chain[0] += 1
                ins.then_inc(chain, 1)
                dve.wait_ge(chain, n_chain[0])

            dve.memset(minus_half[:], -0.5).then_inc(eps_set, 1)
            dve.memset(eps_ln[:], EPS_LN).then_inc(eps_set, 1)
            dve.memset(zeros[:], 0.0).then_inc(pads_set, 1)
            dve.memset(at_p[:, :, :, :, CHUNK:CW].bitcast(F32), 0.0).then_inc(pads_set, 1)

            def x_moments(k):
                dve.wait_ge(x_loaded[k], 16)
                for n in range(k * BT, (k + 1) * BT):
                    dve.bn_stats(stats[:, n, :], x_all[:, n, :]).then_inc(x_stats, 1)
                for n in range(k * BT, (k + 1) * BT):
                    dve.wait_ge(x_stats, n + 1)
                    dve.bn_aggr(mv_in[:, n, :], stats[:, n, :]).then_inc(x_var, 1)

            def norm_x(k):
                dve.wait_ge(x_rstd, k + 1)
                if k >= 2:
                    dve.wait_ge(hs_transposed, k - 1)
                for j in range(BT):
                    n = k * BT + j
                    dve.tensor_scalar(hs[:, k % 2, j, :], x_all[:, n, :], mv_in[:, n, 0:1], rstd[:, n:n + 1],
                                      ALU.subtract, ALU.mult).then_inc(hs_ready, 1)

            def normed_lo(k):
                for kc in range(KC):
                    dve.wait_ge(hst_hi, KC * k + kc + 1)
                    dve.tensor_tensor(hst_p[:, k % 2, 1, kc], tps(kc, 0, BT * P), hst_p[:, k % 2, 0, kc].bitcast(F32),
                                      ALU.subtract).then_inc(hst_lo, 1)

            def split_query_weights():
                dve.wait_ge(wq_loaded, 16)
                raw_g = w_raw[:].rearrange("p k (g c) -> p k g c", g=G)
                for twin in range(2):
                    dve.tensor_copy(wq_p[:, 0, :, :, twin, :], raw_g).then_inc(wq_split, 1)
                dve.wait_ge(wq_split, 2)
                for twin in range(2):
                    for kc in range(KC):
                        dve.tensor_tensor(wq_p[:, 1, kc, :, twin, :], raw_g[:, kc],
                                          wq_p[:, 0, kc, :, twin, :].bitcast(F32), ALU.subtract).then_inc(wq_split, 1)

            def split_key_value_weights():
                dve.tensor_copy(wk_p[:, 0], w_raw2[:]).then_inc(w_split, 1)
                dve.tensor_copy(wv_p[:, 0], w_raw3[:]).then_inc(w_split, 1)
                dve.wait_ge(w_split, 2)
                dve.tensor_tensor(wk_p[:, 1], w_raw2[:], wk_p[:, 0].bitcast(F32), ALU.subtract).then_inc(w_split, 1)
                dve.tensor_tensor(wv_p[:, 1], w_raw3[:], wv_p[:, 0].bitcast(F32), ALU.subtract).then_inc(w_split, 1)

            def make_masks():
                inv = 1.0 / float(np.sqrt(HD))
                for t in range(NKT):
                    linked(dve.tensor_scalar(m_scale[0:KEYS[t], t], mask_i[0:KEYS[t], t], 0.5, inv, ALU.is_gt,
                                             ALU.mult))
                    dve.tensor_scalar(m_bias[0:KEYS[t], t], m_scale[0:KEYS[t], t], SCORE_CLIP / inv, -SCORE_CLIP,
                                      ALU.mult, ALU.add).then_inc(mask_ready, 1)

            def apply_gates():
                dve.wait_ge(gates_ready, 2)
                dve.tensor_scalar(rsc[:], scal[:, 2:3], 0.0, RES_SCALE_MAX, ALU.max, ALU.min).then_inc(rsc_ready, 1)
                for v in (gam, bet):
                    dve.tensor_scalar(v[:], v[:], tg[:, 0:1], None, ALU.mult).then_inc(gates_applied, 1)

            def split_hi(g, c):
                s = c % 2
                dve.wait_ge(at_loaded[s], (g - s) * 8 + 16)
                if not (isinstance(g, int) and g < 2):
                    dve.wait_ge(v_projected, NKT * (g - 1))
                dve.tensor_copy(at_p[:, s, 0, :, 0:CHUNK], at_raw[:, s]).then_inc(at_split, 1)

            def split_lo(g, c):
                s = c % 2
                dve.wait_ge(at_split, g * 2 + 1)
                dve.tensor_tensor(at_p[:, s, 1, :, 0:CHUNK], at_raw[:, s], at_p[:, s, 0, :, 0:CHUNK].bitcast(F32),
                                  ALU.subtract).then_inc(at_split, 1)

            def key_lo(g, c, m):
                for h in range(2):
                    grp = 2 * m + h
                    dve.wait_ge(k_hi, g * G + grp + 1)
                    dve.scalar_tensor_tensor(out=kt_p[GR:P, c % 2, grp, :], in0=kps(m)[h * GR:(h + 1) * GR],
                                             scalar=bk_sb[h * GR:(h + 1) * GR, m:m + 1],
                                             in1=kt_p[0:GR, c % 2, grp, :].bitcast(F32),
                                             op0=ALU.add, op1=ALU.subtract).then_inc(k_lo, 1)

            def value_tile(g, c, t):
                dve.wait_ge(v_projected, g * NKT + t + 1)
                if not (isinstance(g, int) and g < 2):
                    dve.wait_ge(pv_done, (g - 2) * UPC + 2 * t + 2)
                n = KEYS[t]
                dve.tensor_tensor(v_sb[0:n, c % 2, t, :, 0:HD], vps[0:n].rearrange("p (h d) -> p h d", h=H),
                                  bv_sb[0:n].rearrange("p (h d) -> p h d", h=H), ALU.add).then_inc(v_ready, 1)

            def clip(U, u):
                dve.wait_ge(exped, U + 1)
                n = KEYS[(u % UPC) // 2]
                e = ex[0:n, u % NE]
                dve.tensor_scalar(e, e, EXP_LO, EXP_HI, ALU.max, ALU.min).then_inc(clipped, 1)

            def attend(b, last_batch):
                for u in range(UPB):
                    c, v = divmod(u, UPC)
                    g = b * CPB + c
                    more = not (last_batch and c == CPB - 1)
                    tile, after = VALUES_AT.get(v, (None, None))
                    if tile is not None and not after and more:
                        value_tile(g + 1, c + 1, tile)
                    clip(b * UPB + u, u)
                    if v < 2 and more:
                        key_lo(g + 1, c + 1, v)
                    if tile is not None and after and more:
                        value_tile(g + 1, c + 1, tile)
                    if not (last_batch and c >= CPB - 2):
                        if v == 2:
                            split_hi(g + 2, c)
                        if v == 4:
                            split_lo(g + 2, c)
            x_moments(0)
            x_moments(1)
            norm_x(0)
            split_query_weights()
            normed_lo(0)
            norm_x(1)
            x_moments(2)
            dve.wait_ge(params_loaded, 16 * NPARAM)
            split_key_value_weights()
            x_moments(3)
            norm_x(2)
            normed_lo(1)
            make_masks()
            apply_gates()
            x_moments(4)
            norm_x(3)
            normed_lo(2)
            norm_x(4)
            normed_lo(3)
            for g in range(2):
                split_hi(g, g)
                split_lo(g, g)
            normed_lo(4)
            dve.wait_ge(q_stored, G * NBLK)
            dve.memset(v_sb[:, :, :, :, HD:VW], 1.0).then_inc(pads_set, 1)
            key_lo(0, 0, 0)
            key_lo(0, 0, 1)
            for t in range(NKT):
                value_tile(0, 0, t)
            attend(0, False)
            with dve.Fori(1, B - 1) as b:
                attend(b, False)
            attend(B - 1, True)

            def eps_times_sum(i, slot):
                dve.wait_ge(stage_transposed, i + 1)
                dve.tensor_scalar(den[:, 0, slot], sums(slot), EPS_PROBS, None, ALU.mult).then_inc(eps_sums, 1)

            def sums(slot):
                return ps[:, slot].rearrange("p (h c) -> p h c", c=32)[:, :, HD]

            def denominator(i, slot):
                dve.wait_ge(eps_sums, i + 1)
                dve.tensor_tensor(den[:, 1, slot], sums(slot), den[:, 0, slot], ALU.add).then_inc(den_ready, 1)

            def factor(i, slot):
                dve.wait_ge(den_ready, i + 1)
                dve.reciprocal(den[:, 2, slot], den[:, 1, slot]).then_inc(recip_ready, 1)

            def norm_ctx(i, slot):
                dve.wait_ge(recip_ready, i + 1)
                used(dve, ctxn_transposed, i - 1)
                dve.tensor_tensor(ctxn[:, slot].rearrange("p (h d) -> p h d", h=H),
                                  ps[:, slot].rearrange("p (h c) -> p h c", c=32)[:, :, 0:HD],
                                  den[:, 2, slot].unsqueeze(2).to_broadcast([P, H, HD]), ALU.mult
                                  ).then_inc(ctx_normed, 1)

            def stats_of_delta(i, slot):
                dve.wait_ge(delta_ready, i + 1)
                dve.bn_stats(st_d[:, slot], dlt[:, slot]).then_inc(delta_stats, 1)

            def var_of_delta(i, slot):
                dve.wait_ge(delta_stats, i + 1)
                used(dve, roots_ready, i - 1)
                used(dve, zed_ready, i - 1)
                dve.nop(nofuse=True)
                dve.bn_aggr(mv[:, slot, 0], st_d[:, slot]).then_inc(delta_var, 1)

            def centre_delta(i, slot):
                dve.wait_ge(delta_var, i + 1)
                dve.scalar_tensor_tensor(out=zed[:, slot], in0=dlt[:, slot], scalar=mv[:, slot, 0, 0:1], in1=gam[:],
                                         op0=ALU.subtract, op1=ALU.mult).then_inc(zed_ready, 1)

            def first_residual(i, slot):
                dve.wait_ge(zed_ready, i + 1)
                dve.wait_ge(roots_ready, i + 1)
                dve.wait_ge(beta_added, NT)
                dve.scalar_tensor_tensor(out=one(x_all, i), in0=zed[:, slot], scalar=rstds[:, slot, 0:1],
                                         in1=one(x_all, i), op0=ALU.mult, op1=ALU.add).then_inc(x1_ready, 1)

            def stats_of_x1(i, slot):
                dve.wait_ge(x1_ready, i + 1)
                dve.nop(nofuse=True)
                dve.bn_stats(st_x[:, slot], one(x_all, i)).then_inc(x1_stats, 1)

            def var_of_x1(i, slot):
                dve.wait_ge(x1_stats, i + 1)
                used(dve, roots_ready, i + X1_ROOT - DELTA_ROOT - 1)
                used(dve, xn_ready, i - 1)
                dve.nop(nofuse=True)
                dve.bn_aggr(mv[:, slot, 1], st_x[:, slot]).then_inc(x1_var, 1)

            def norm_x1(i, slot):
                dve.wait_ge(roots_ready, i + X1_ROOT - DELTA_ROOT + 1)
                used(dve, xn_transposed, i - 1)
                dve.tensor_scalar(xn[:, slot], one(x_all, i), mv[:, slot, 1, 0:1], rstds[:, slot, 1:2],
                                  ALU.subtract, ALU.mult).then_inc(xn_ready, 1)

            def keep_logits(i, slot):
                dve.wait_ge(logits_done, i + 1)
                dve.tensor_copy(one(lg, i), ps[:, 6 + slot, D:D + E]).then_inc(logits_kept, 1)

            def step(t, slot):
                plan = ((10, keep_logits), (2, eps_times_sum), (5, stats_of_delta), (X1_ROOT, var_of_x1),
                        (2, denominator), (6, centre_delta), (2, factor), (DELTA_ROOT, var_of_delta),
                        (6, first_residual), (2, norm_ctx), (8, norm_x1), (6, stats_of_x1))
                for behind, work in plan:
                    if exists(t - behind):
                        work(t - behind, (slot - behind) % 2)
            tile_steps(dve, step)

            dve.wait_ge(logits_kept, NT)
            dve.wait_ge(w_lo, NPIECE)

            def input_lo(i, slot):
                dve.wait_ge(xs_hi, i + 1)
                dve.tensor_tensor(xs_p[:, slot, 1], tile_cols(qc[:, 2:4], i), xs_p[:, slot, 0].bitcast(F32),
                                  ALU.subtract).then_inc(xs_lo, 1)

            input_lo(0, 0)
            for e in range(E):
                dve.memset(iota_e[:, :, e:e + 1], float(e))
            m1, m2, first_e, wgt = (r_m[:, q] for q in range(4))

            def wide(m):
                return m.unsqueeze(2).to_broadcast([P, NT, E])
            linked(dve.tensor_reduce(m1, lg[:], AX_X, ALU.max))
            linked(dve.tensor_tensor(r_a[:], lg[:], wide(m1), ALU.not_equal))
            linked(dve.scalar_tensor_tensor(out=r_b[:], in0=r_a[:], scalar=float(E), in1=iota_e[:], op0=ALU.mult,
                                            op1=ALU.add))
            linked(dve.tensor_reduce(first_e, r_b[:], AX_X, ALU.min))
            linked(dve.tensor_tensor(r_a[:], iota_e[:], wide(first_e), ALU.is_equal))
            linked(dve.scalar_tensor_tensor(out=r_b[:], in0=r_a[:], scalar=-3.0e38, in1=lg[:], op0=ALU.mult,
                                            op1=ALU.add))
            linked(dve.tensor_reduce(m2, r_b[:], AX_X, ALU.max))
            linked(dve.tensor_tensor(first_e, m2, m1, ALU.subtract))
            dve.tensor_copy(m2, first_e).then_inc(gap_ready, 1)
            dve.wait_ge(gap_exped, 1)
            linked(dve.tensor_scalar(wgt, wgt, 1.0, None, ALU.add))
            linked(dve.reciprocal(wgt, wgt))
            dve.tensor_tensor(lg[:], r_a[:], wide(wgt), ALU.mult).then_inc(combine_ready, 1)

            dve.wait_ge(combine_ready, 1)

            def hidden(i, slot, e):
                dve.wait_ge(silu_done, i * E + e + 1)
                col = lg[:, i, e:e + 1] if isinstance(i, int) else \
                    lg[:, bass.ds(i, 1), e:e + 1].rearrange("p o n -> p (o n)")
                dve.scalar_tensor_tensor(out=act[:, slot, e * I:(e + 1) * I], in0=sil[:, e % 2], scalar=col,
                                         in1=gu_ps(e)[:, I:2 * I], op0=ALU.mult, op1=ALU.mult).then_inc(act_ready, 1)

            def hidden_lo(i, q):
                n = min(4, NF - 4 * q)
                dve.wait_ge(actt_hi, i * 3 + q + 1)
                dve.tensor_tensor(actt_p[:, 1, 4 * q:4 * q + n].rearrange("p f n -> p (f n)"), ps[:, 2 + q, 0:n * P],
                                  actt_p[:, 0, 4 * q:4 * q + n].rearrange("p f n -> p (f n)").bitcast(F32),
                                  ALU.subtract).then_inc(actt_lo, 1)

            def finish(i, slot):
                dve.wait_ge(down_done, i + 1)
                if isinstance(i, int):
                    if i >= 2:
                        dve.wait_ge(y_stored[slot], 16 * (i // 2))
                else:
                    dve.wait_ge(y_stored[slot], (i - slot) * 8)
                dve.scalar_tensor_tensor(out=y_out[:, slot], in0=ps[:, 5, 0:D], scalar=tg[:, 1:2], in1=one(x_all, i),
                                         op0=ALU.mult, op1=ALU.add).then_inc(y_ready, 1)

            def expert_tile(i, slot, has_before, has_next):
                if has_next:
                    input_lo(i + 1, 1 - slot)
                for e in range(E):
                    hidden(i, slot, e)
                    if has_before:
                        if 2 <= e < 5:
                            hidden_lo(i - 1, e - 2)
                        if e == 7:
                            finish(i - 1, 1 - slot)
            expert_tile(0, 0, False, True)
            expert_tile(1, 1, True, True)
            with dve.Fori(1, NT // 2) as r:
                expert_tile(r * 2, 0, True, True)
                expert_tile(r * 2 + 1, 1, True, True)
            expert_tile(NT - 1, 0, True, False)
            for q in range(3):
                hidden_lo(NT - 1, q)
            finish(NT - 1, 0)

        @block.scalar
        def _(ac):
            for dst, src in ((bq_sb, bq), (bk_sb, bk), (rw_sb, router), (wo_sb, wo)):
                ac.dma_start(dst[:], src).then_inc(params_loaded, 16)
            for dst, src in ((bv_sb, bv), (bo_sb, bo), (gam, gamma), (bet, beta)):
                ac.dma_start(dst[:], src.partition_broadcast(P)).then_inc(params_loaded, 16)
            for k, src in enumerate((g_xattn, g_ffn, rs)):
                ac.dma_start(scal[:, k:k + 1], src.partition_broadcast(P)).then_inc(params_loaded, 16)

            def normed_hi(k):
                for kc in range(KC):
                    ac.wait_ge(hs_transposed, k + 1)
                    if k >= 2:
                        ac.wait_ge(q_projected, G * (k - 1))
                    ac.copy(hst_p[:, k % 2, 0, kc], tps(kc, 0, BT * P)).then_inc(hst_hi, 1)

            def store_queries(k):
                for g in range(G):
                    ac.wait_ge(q_projected, G * k + g + 1)
                    ac.activation(qc[:, g, k * BT * P:(k + 1) * BT * P].rearrange("p (h n) -> p h n", h=2),
                                  ps[:, 4 + 2 * (g % 2):6 + 2 * (g % 2), 0:BT * P // 2], ACT.Identity,
                                  bias=bq_sb[:, g:g + 1]).then_inc(q_stored, 1)
                    if g == 1 and k + 1 < NBLK:
                        normed_hi(k + 1)
            normed_hi(0)
            ac.wait_ge(params_loaded, 16 * NPARAM)
            for k in range(2):
                ac.activation(tg[:, k:k + 1], scal[:, k:k + 1], ACT.Tanh).then_inc(gates_ready, 1)
            for k in range(NBLK):
                store_queries(k)

            ac.wait_ge(mask_ready, NKT)
            ac.wait_ge(q_stored, G * NBLK)

            def key_hi(g, c, m):
                ac.wait_ge(k_projected, g * 2 + m + 1)
                if not (isinstance(g, int) and g < 2):
                    ac.wait_ge(scored, g * UPC - UPC)
                for h in range(2):
                    ac.activation(kt_p[0:GR, c % 2, 2 * m + h, :], kps(m)[h * GR:(h + 1) * GR], ACT.Identity,
                                  bias=bk_sb[h * GR:(h + 1) * GR, m:m + 1]).then_inc(k_hi, 1)

            def column(tab, n, t, g):
                return tab[0:n, t, g:g + 1] if isinstance(g, int) else tab[0:n, t, bass.ds(g, 1)]

            def expo(b, u, g):
                n, t = KEYS[(u % UPC) // 2], (u % UPC) // 2
                U = b * UPB + u
                ac.wait_ge(scored, U + 1)
                if not (isinstance(b, int) and b * UPB + u < NE):
                    ac.wait_ge(pv_done, U - (NE - 1))
                ac.nop(nofuse=True)
                ac.activation(ex[0:n, u % NE], sps(u)[0:n], ACT.Exp, bias=column(m_bias, n, t, g),
                              scale=column(m_scale, n, t, g)).then_inc(exped, 1)

            def save_ctx(b):
                ac.wait_ge(pv_done, b * UPB + UPB)
                ac.wait_ge(q_built, b * G + G)
                dst = qc[:, :, b * S:(b + 1) * S] if isinstance(b, int) else qc[:, :, bass.ds(b * S, S)]
                ac.copy(dst, ctx_ps.rearrange("p (g s) -> p g s", g=G)).then_inc(ctx_saved, 1)

            def attend(b, first_batch, last_batch):
                for u in range(UPB):
                    c, v = divmod(u, UPC)
                    g = b * CPB + c
                    expo(b, u, g)
                    if v < 2 and not (last_batch and c == CPB - 1):
                        key_hi(g + 1, c + 1, v)
                    if u == 1 and not first_batch:
                        save_ctx(b - 1)
            key_hi(0, 0, 0)
            key_hi(0, 0, 1)
            attend(0, True, False)
            with ac.Fori(1, B - 1) as b:
                attend(b, False, False)
            attend(B - 1, False, True)
            save_ctx(B - 1)

            def stage(i, slot):
                used(ac, stage_transposed, i - 1)
                if isinstance(i, int):
                    ac.wait_ge(ctx_saved, B)
                ac.copy(stg[:, slot], tile_cols(qc, i)).then_inc(staged, 1)

            def transposed_ctx(i, slot):
                ac.wait_ge(ctxn_transposed, i + 1)
                used(ac, o_projected, i - 1)
                ac.copy(ctxt[:, slot].rearrange("p k n -> p (k n)"), ps[:, 2 + slot, 0:D]).then_inc(ctxt_ready, 1)

            def scaled_delta(i, slot):
                ac.wait_ge(o_projected, i + 1)
                used(ac, zed_ready, i - 1)
                ac.activation(dlt[:, slot], ps[:, 4 + slot, 0:D], ACT.Copy, scale=rsc[:, 0:1]
                              ).then_inc(delta_ready, 1)

            def transposed_xn(i, slot):
                ac.wait_ge(xn_transposed, i + 1)
                used(ac, logits_done, i - 1)
                src = ps[:, 6 + slot, 0:D].rearrange("p (k n) -> p k n", k=KC)
                ac.copy(xts[:, slot], src).then_inc(xts_ready, 1)
                ac.copy(tile_cols(qc[:, 2:4], i), src).then_inc(xt_kept, 1)

            def split_high(k):
                if isinstance(k, int):
                    ac.wait_ge(w_loaded[k * LOADS // NPIECE], 16)
                ac.copy(piece(0, k), one(w_in, k)).then_inc(w_hi, 1)

            def step(t, slot):
                for behind, work in ((0, stage), (4, scaled_delta), (2, transposed_ctx), (8, transposed_xn)):
                    if exists(t - behind):
                        work(t - behind, (slot - behind) % 2)
                k = piece_of_step(t, slot)
                if k is not None:
                    if not isinstance(k, int):
                        for n in range(LOADS):
                            ac.wait_ge(w_loaded[n], 16)
                    split_high(k)
            tile_steps(ac, step)
            ac.wait_ge(w_lo, NPIECE)

            ac.wait_ge(xt_kept, NT)

            def input_hi(i, slot):
                if not (isinstance(i, int) and i < 2):
                    ac.wait_ge(gu_done, i * E - E)
                src = qc[:, 2:4, i * P:(i + 1) * P] if isinstance(i, int) else qc[:, 2:4, bass.ds(i * P, P)]
                ac.copy(xs_p[:, slot, 0], src).then_inc(xs_hi, 1)

            def silu(i, slot, e):
                ac.wait_ge(gu_done, i * E + e + 1)
                if not (isinstance(i, int) and i == 0 and e < 2):
                    ac.wait_ge(act_ready, i * E + e - 1)
                ac.activation(sil[:, e % 2], gu_ps(e)[:, 0:I], ACT.Silu).then_inc(silu_done, 1)

            def hidden_hi(i, q):
                n = min(4, NF - 4 * q)
                ac.wait_ge(act_transposed, i * 3 + q + 1)
                if not (isinstance(i, int) and i == 0):
                    ac.wait_ge(down_done, i)
                ac.copy(actt_p[:, 0, 4 * q:4 * q + n].rearrange("p f n -> p (f n)"), ps[:, 2 + q, 0:n * P]
                        ).then_inc(actt_hi, 1)

            def expert_tile(i, slot, has_before, has_next):
                if has_next:
                    input_hi(i + 1, 1 - slot)
                for e in range(E):
                    silu(i, slot, e)
                    if has_before and 2 <= e < 5:
                        hidden_hi(i - 1, e - 2)
            input_hi(0, 0)
            ac.wait_ge(gap_ready, 1)
            ac.activation(r_m[:, 3], r_m[:, 1], ACT.Exp).then_inc(gap_exped, 1)
            expert_tile(0, 0, False, True)
            expert_tile(1, 1, True, True)
            with ac.Fori(1, NT // 2) as r:
                expert_tile(r * 2, 0, True, True)
                expert_tile(r * 2 + 1, 1, True, True)
            expert_tile(NT - 1, 0, True, False)
            for q in range(3):
                hidden_hi(NT - 1, q)

        @block.tensor
        def _(pe):
            def parts(dst, lhs, rhs, rounds):
                last = None
                todo = [(k, a, b) for k in range(rounds) for a, b in ((0, 0), (0, 1), (1, 0))]
                for q, (k, a, b) in enumerate(todo):
                    last = pe.matmul(dst, lhs(a, k), rhs(b, k), start=q == 0, stop=q == len(todo) - 1)
                return last

            pe.wait_ge(consts_made, 1)

            def transpose_normed(k):
                if k >= 1:
                    pe.wait_ge(hst_lo, KC * k)
                for j in range(BT):
                    pe.wait_ge(hs_ready, BT * k + j + 1)
                    for kc in range(KC):
                        last = pe.transpose(tps(kc, j * P, P), hs[:, k % 2, j, kc * P:(kc + 1) * P], ident[:])
                last.then_inc(hs_transposed, 1)

            def project_queries(k):
                pe.wait_ge(hst_lo, KC * (k + 1))
                for g in range(G):
                    n = G * k + g
                    if n >= 2:
                        pe.wait_ge(q_stored, n - 1)
                    for half in range(2):
                        w = BT * P // 2
                        last = parts(qps(g, half),
                                     lambda p, kc: wq_p[:, p, kc, g].rearrange("p t c -> p (t c)"),
                                     lambda p, kc: hst_p[:, k % 2, p, kc, half * w:(half + 1) * w], KC)
                    last.then_inc(q_projected, 1)
                    if g == 1 and k + 1 < NBLK:
                        transpose_normed(k + 1)
            transpose_normed(0)
            pe.wait_ge(wq_split, 2 + 2 * KC)
            for k in range(NBLK):
                project_queries(k)

            pe.wait_ge(w_split, 4)
            pe.wait_ge(pads_set, 2)
            pe.matmul(ps[:, 3, :], zeros[:, 0:P], zeros[:], start=True, stop=True).then_inc(ctx_cleared, 1)

            def project_keys(g, c, m):
                pe.wait_ge(at_split, g * 2 + 2)
                if not (isinstance(g, int) and g < 1):
                    pe.wait_ge(k_lo, g * G - G + 2 * m + 2)
                s = c % 2
                parts(kps(m), lambda p, kc: wk_p[:, p, kc, m * P:(m + 1) * P], lambda p, kc: at_p[:, s, p, kc, :],
                      KC).then_inc(k_projected, 1)

            def project_values(g, c, t):
                if not (isinstance(g, int) and g * NKT + t < 1):
                    pe.wait_ge(v_ready, g * NKT + t)
                s, o, n = c % 2, KOFF[t], KEYS[t]
                parts(vps[0:n], lambda p, kc: at_p[:, s, p, kc, o:o + n], lambda p, kc: wv_p[:, p, kc, :],
                      KC).then_inc(v_projected, 1)

            def scores(b, u, g):
                v = u % UPC
                t, half = v // 2, v % 2
                o, n = KOFF[t], KEYS[t]
                U = b * UPB + u
                if not (isinstance(b, int) and b == 0 and u < 2):
                    pe.wait_ge(exped, U - 1)
                if t == 0:
                    pe.wait_ge(k_lo, g * G + 2 * half + 2)
                if u == 0:
                    pe.wait_ge(q_built, b * G + G)
                last = None
                for h in range(2):
                    grp = 2 * half + h
                    for part in range(2):
                        q = qbd[:, b % 2, part, grp] if isinstance(b, int) else \
                            qbd[:, bass.ds(b % 2, 1), part, grp].rearrange("p o h s -> p (o h) s")
                        last = pe.matmul(sps(u)[0:n, h], kt_p[:, (u // UPC) % 2, grp, o:o + n],
                                         q, start=part == 0, stop=part == 1)
                last.then_inc(scored, 1)

            def weigh_values(b, u):
                v = u % UPC
                c, t, half = u // UPC, v // 2, v % 2
                n = KEYS[t]
                U = b * UPB + u
                pe.wait_ge(clipped, U + 1)
                if half == 0:
                    pe.wait_ge(v_ready, (b * CPB + c) * NKT + t + 1)
                if u == 0 and not (isinstance(b, int) and b == 0):
                    pe.wait_ge(ctx_saved, b)
                last = None
                for q in range(2 * HG):
                    h = 2 * HG * half + q
                    s, j = h // HG, h % HG
                    last = pe.matmul(ctx_ps[32 * j:32 * j + VW, s * S:(s + 1) * S], v_sb[0:n, c % 2, t, h, :],
                                     ex[0:n, u % NE, q // HG, j * S:(j + 1) * S],
                                     start=u == 0 and s == 0, stop=u >= UPB - 2 and s == 2 * half + 1,
                                     skip_group_check=True)
                last.then_inc(pv_done, 1)

            def attend(b, first_batch, last_batch):
                for u in range(UPB):
                    c, v = divmod(u, UPC)
                    g = b * CPB + c
                    more = not (last_batch and c == CPB - 1)
                    scores(b, u, g)
                    if v < 2 and more:
                        project_keys(g + 1, c + 1, v)
                    tile, after = VALUES_AT.get(v, (None, None))
                    if tile is not None and not after and more:
                        project_values(g + 1, c + 1, tile)
                    if u % PVG == 1:
                        for w in range(u - 1 - PVG, u - 1):
                            if w >= 0:
                                weigh_values(b, w)
                            elif not first_batch:
                                weigh_values(b - 1, w + UPB)
                    if tile is not None and after and more:
                        project_values(g + 1, c + 1, tile)
            project_keys(0, 0, 0)
            project_keys(0, 0, 1)
            for t in range(NKT):
                project_values(0, 0, t)
            pe.wait_ge(pads_set, 3)
            pe.wait_ge(q_stored, G * NBLK)
            attend(0, True, False)
            with pe.Fori(1, B - 1) as b:
                attend(b, False, False)
            attend(B - 1, False, True)
            for u in range(UPB - PVG, UPB):
                weigh_values(B - 1, u)

            pe.wait_ge(params_loaded, 16 * NPARAM)

            def transpose_stage(i, slot):
                pe.wait_ge(staged, i + 1)
                used(pe, ctx_normed, i - 1)
                for g in range(G):
                    last = pe.transpose(ps[:, slot, g * P:(g + 1) * P], stg[:, slot, g], ident[:])
                last.then_inc(stage_transposed, 1)

            def transpose_ctx(i, slot):
                pe.wait_ge(ctx_normed, i + 1)
                used(pe, ctxt_ready, i - 1)
                for kc in range(KC):
                    last = pe.transpose(ps[:, 2 + slot, kc * P:(kc + 1) * P], ctxn[:, slot, kc * P:(kc + 1) * P],
                                        ident[:])
                last.then_inc(ctxn_transposed, 1)

            def project_ctx(i, slot):
                pe.wait_ge(ctxt_ready, i + 1)
                used(pe, delta_ready, i - 1)
                dst = ps[:, 4 + slot, 0:D]
                for kc in range(KC):
                    pe.matmul(dst, ctxt[:, slot, kc], wo_sb[:, kc], start=kc == 0, stop=False)
                pe.matmul(dst, ident[:], bo_sb[:], start=False, stop=True).then_inc(o_projected, 1)

            def transpose_xn(i, slot):
                pe.wait_ge(xn_ready, i + 1)
                used(pe, logits_kept, i - 1)
                for kc in range(KC):
                    last = pe.transpose(ps[:, 6 + slot, kc * P:(kc + 1) * P], xn[:, slot, kc * P:(kc + 1) * P],
                                        ident[:])
                last.then_inc(xn_transposed, 1)

            def logits(i, slot):
                pe.wait_ge(xts_ready, i + 1)
                pe.wait_ge(xt_kept, i + 1)
                for kc in range(KC):
                    last = pe.matmul(ps[:, 6 + slot, D:D + E], xts[:, slot, kc], rw_sb[:, kc], start=kc == 0,
                                     stop=kc == KC - 1)
                last.then_inc(logits_done, 1)

            def step(t, slot):
                plan = ((1, transpose_stage), (4, project_ctx), (9, logits), (2, transpose_ctx), (8, transpose_xn))
                for behind, work in plan:
                    if exists(t - behind):
                        work(t - behind, (slot - behind) % 2)
            tile_steps(pe, step)

            pe.wait_ge(xt_kept, NT)
            pe.wait_ge(logits_kept, NT)
            pe.wait_ge(w_lo, NPIECE)

            def gate_up(i, slot, e):
                if not (isinstance(i, int) and i == 0 and e < 4):
                    pe.wait_ge(act_ready, i * E + e - 3)
                parts(gu_ps(e)[:, 0:2 * I], lambda p, kc: xs_p[:, slot, p, kc, :],
                      lambda p, kc: gu_w(p, kc, e), KC).then_inc(gu_done, 1)

            def transpose_hidden(i, slot, q):
                if q == 0:
                    pe.wait_ge(act_ready, i * E + E)
                if not (isinstance(i, int) and i == 0):
                    pe.wait_ge(actt_lo, i * 3 - 3 + q + 1)
                n = min(4, NF - 4 * q)
                for f in range(4 * q, 4 * q + n):
                    last = pe.transpose(ps[:, 2 + q, (f % 4) * P:(f % 4 + 1) * P], act[:, slot, f * P:(f + 1) * P],
                                        ident[:])
                last.then_inc(act_transposed, 1)

            def down_proj(i):
                pe.wait_ge(actt_lo, i * 3 + 3)
                if not (isinstance(i, int) and i == 0):
                    pe.wait_ge(y_ready, i)
                parts(ps[:, 5, 0:D], lambda p, f: actt_p[:, p, f, :], dn_w,
                      NF).then_inc(down_done, 1)

            def expert_tile(i, slot, has_before):
                pe.wait_ge(xs_lo, i + 1)
                for e in range(E):
                    gate_up(i, slot, e)
                    if has_before and 1 <= e < 4:
                        transpose_hidden(i - 1, 1 - slot, e - 1)
                    if has_before and e == 6:
                        down_proj(i - 1)
            expert_tile(0, 0, False)
            expert_tile(1, 1, True)
            with pe.Fori(1, NT // 2) as r:
                expert_tile(r * 2, 0, True)
                expert_tile(r * 2 + 1, 1, True)
            expert_tile(NT - 1, 0, True)
            for q in range(3):
                transpose_hidden(NT - 1, 0, q)
            down_proj(NT - 1)


def kernel(x, ctx_2048, mask_BxS2_ik0, g_xattn, g_ffn, L0_xattn_Wq, L0_xattn_bq, L0_xattn_Wk, L0_xattn_bk,
           L0_xattn_Wv, L0_xattn_bv, L0_xattn_Wo, L0_xattn_bo, L0_xattn_ln_gamma, L0_xattn_ln_beta,
           L0_xattn_residual_scale, L0_ffn_router_w, L0_ffn_gate_w, L0_ffn_up_w, L0_ffn_down_w):
    import concourse.bacc as bacc
    from concourse.bass_utils import run_bass_kernel_spmd

    def lay(a):
        return np.ascontiguousarray(a)

    def weight(w):
        w = np.asarray(w)
        return lay(w.T.reshape(KC, P, w.shape[0]).transpose(1, 0, 2))

    def experts_in(w):
        return np.asarray(w).transpose(2, 0, 1).reshape(KC, P, E, I).transpose(1, 0, 2, 3)

    gate_up = np.concatenate([experts_in(L0_ffn_gate_w), experts_in(L0_ffn_up_w)], axis=3)
    down = np.asarray(L0_ffn_down_w).transpose(0, 2, 1).reshape(NF, P, D).transpose(1, 0, 2)
    bq = np.asarray(L0_xattn_bq).reshape(G, GR)
    data = {
        "x": lay(np.asarray(x).reshape(TOK, D)),
        "ctx_t": lay(np.asarray(ctx_2048).reshape(NCH, CHUNK, KC, P).transpose(0, 3, 2, 1)),
        "mask_t": lay(np.asarray(mask_BxS2_ik0).reshape(NCH, CHUNK).T),
        "g_xattn": lay(np.asarray(g_xattn).reshape(1)),
        "g_ffn": lay(np.asarray(g_ffn).reshape(1)),
        "wq": weight(L0_xattn_Wq),
        "bq": lay(np.concatenate([bq, bq], axis=1).T),
        "wk": weight(L0_xattn_Wk),
        "bk": lay(np.asarray(L0_xattn_bk).reshape(KC, P).T),
        "wv": weight(L0_xattn_Wv),
        "bv": lay(L0_xattn_bv),
        "wo": weight(L0_xattn_Wo),
        "bo": lay(L0_xattn_bo),
        "gamma": lay(L0_xattn_ln_gamma),
        "beta": lay(L0_xattn_ln_beta),
        "rs": lay(np.asarray(L0_xattn_residual_scale).reshape(1)),
        "router": weight(L0_ffn_router_w),
        "w_ffn": lay(np.concatenate([gate_up.reshape(P, -1), down.reshape(P, -1)], axis=1).reshape(P, NPIECE, PIECE)),
    }
    nc = bacc.Bacc("TRN2", target_bir_lowering=False, num_devices=1)
    args = [nc.dram_tensor(name, a.shape, mybir.dt.from_np(a.dtype), kind="ExternalInput").ap()
            for name, a in data.items()]
    out = nc.dram_tensor("out", (TOK, D), F32, kind="ExternalOutput").ap()
    build(nc, *args, out)
    r = run_bass_kernel_spmd(nc, [data], core_ids=[0])
    return r.results[0]["out"].reshape(B, S, D)
```
